# Optimizing a Trainium2 kernel written in Bass

```python
import numpy as np
import jax
import jax.numpy as jnp

def _softmax(x, axis=-1):
    return jax.nn.softmax(x, axis=axis)

def _gelu(x):
    return jax.nn.gelu(x, approximate=True)

def _silu(x):
    return jax.nn.silu(x)

def _sigmoid(x):
    return jax.nn.sigmoid(x)

def _layernorm(x, axis=-1, eps=1e-05):
    m = jnp.mean(x, axis=axis, keepdims=True)
    v = jnp.var(x, axis=axis, keepdims=True)
    return (x - m) / jnp.sqrt(v + eps)

def _scatter_add(tgt, idx, src, axis=0):
    return tgt.at[idx].add(src)

def _segment_sum(src, seg, n):
    return jax.ops.segment_sum(src, seg, n)
kernel_name = 'mk_conv_preact_d2_conv_nchw512_r4_0d3fc5'

def setup_inputs(seed: int=0):
    np.random.seed(seed)
    _w = jnp.asarray

    def _rec_inputs():
        import jax
        import jax.numpy as jnp
        _gk = jax.random.key(seed)
        x = -0.000125 + 0.9999 * jax.random.normal(jax.random.fold_in(_gk, 1), (16, 128, 16, 16), jnp.float32)
        return x
    x = _rec_inputs()

    def _L0_conv_setup():
        import jax, jax.numpy as jnp
        import numpy as np
        B, DIM, H, W = (16, 128, 16, 16)
        HEADS, DH = (8, 16)
        INNER = HEADS * DH
        EPS = 1e-05

        def chan_ln(x, g):
            mean = jnp.mean(x, axis=1, keepdims=True)
            var = jnp.var(x, axis=1, keepdims=True)
            return (x - mean) * jax.lax.rsqrt(var + EPS) * g[None, :, None, None]

        def depthwise3x3(x, w):
            return jax.lax.conv_general_dilated(x, w, window_strides=(1, 1), padding='SAME', feature_group_count=x.shape[1], dimension_numbers=('NCHW', 'OIHW', 'NCHW'))
        key = jax.random.key(seed)
        ks = jax.random.split(key, 8)

        def w(k, shape, scale=0.05):
            return jax.random.normal(k, shape, dtype=jnp.float32) * scale
        return {'fmap': jax.random.normal(ks[0], (B, DIM, H, W), dtype=jnp.float32), 'g_norm': jnp.ones((DIM,), jnp.float32), 'q_w1': w(ks[1], (INNER, DIM)), 'q_dw': w(ks[2], (INNER, 1, 3, 3)), 'k_w1': w(ks[3], (INNER, DIM)), 'k_dw': w(ks[4], (INNER, 1, 3, 3)), 'v_w1': w(ks[5], (INNER, DIM)), 'v_dw': w(ks[6], (INNER, 1, 3, 3)), 'out_w': w(ks[7], (DIM, INNER)), 'g_out': jnp.ones((DIM,), jnp.float32)}
    _L0_conv_all = _L0_conv_setup()
    _L0_conv_in = {k: v for k, v in _L0_conv_all.items() if k in ('g_norm', 'q_w1', 'q_dw', 'k_w1', 'k_dw', 'v_w1', 'v_dw', 'out_w', 'g_out')}
    del _L0_conv_all

    def _L1_conv_setup():
        import jax, jax.numpy as jnp
        from jax import lax
        import numpy as np
        DIM = 8
        BN_EPS = 1e-05
        ATT_EPS = 1e-15
        key = jax.random.key(seed)
        ks = jax.random.split(key, 6)
        B, C, H, W = (2, 128, 32, 32)
        total_dim = 128
        c3 = 3 * total_dim
        x = jax.random.normal(ks[0], (B, C, H, W), dtype=jnp.float32)
        w_qkv = jax.random.normal(ks[1], (c3, C), dtype=jnp.float32) * 0.02
        w_dw = jax.random.normal(ks[2], (c3, 1, 5, 5), dtype=jnp.float32) * 0.05
        w_pw = jax.random.normal(ks[3], (c3, 8, 1, 1), dtype=jnp.float32) * 0.1
        w_proj = jax.random.normal(ks[4], (128, 2 * total_dim), dtype=jnp.float32) * 0.02
        bn_gamma = jnp.ones((128,), jnp.float32)
        bn_beta = jnp.zeros((128,), jnp.float32)
        bn_mean = jnp.zeros((128,), jnp.float32)
        bn_var = jnp.ones((128,), jnp.float32)
        return {'x': x, 'w_qkv': w_qkv, 'w_dw': w_dw, 'w_pw': w_pw, 'w_proj': w_proj, 'bn_gamma': bn_gamma, 'bn_beta': bn_beta, 'bn_mean': bn_mean, 'bn_var': bn_var}
    _L1_conv_all = _L1_conv_setup()
    _L1_conv_in = {k: v for k, v in _L1_conv_all.items() if k in ('w_qkv', 'w_dw', 'w_pw', 'w_proj', 'bn_gamma', 'bn_beta', 'bn_mean', 'bn_var')}
    del _L1_conv_all
    return {'x': x, 'L0_conv_g_norm': _L0_conv_in['g_norm'], 'L0_conv_q_w1': _L0_conv_in['q_w1'], 'L0_conv_q_dw': _L0_conv_in['q_dw'], 'L0_conv_k_w1': _L0_conv_in['k_w1'], 'L0_conv_k_dw': _L0_conv_in['k_dw'], 'L0_conv_v_w1': _L0_conv_in['v_w1'], 'L0_conv_v_dw': _L0_conv_in['v_dw'], 'L0_conv_out_w': _L0_conv_in['out_w'], 'L0_conv_g_out': _L0_conv_in['g_out'], 'L1_conv_w_qkv': _L1_conv_in['w_qkv'], 'L1_conv_w_dw': _L1_conv_in['w_dw'], 'L1_conv_w_pw': _L1_conv_in['w_pw'], 'L1_conv_w_proj': _L1_conv_in['w_proj'], 'L1_conv_bn_gamma': _L1_conv_in['bn_gamma'], 'L1_conv_bn_beta': _L1_conv_in['bn_beta'], 'L1_conv_bn_mean': _L1_conv_in['bn_mean'], 'L1_conv_bn_var': _L1_conv_in['bn_var']}

def reference(x, L0_conv_g_norm, L0_conv_q_w1, L0_conv_q_dw, L0_conv_k_w1, L0_conv_k_dw, L0_conv_v_w1, L0_conv_v_dw, L0_conv_out_w, L0_conv_g_out, L1_conv_w_qkv, L1_conv_w_dw, L1_conv_w_pw, L1_conv_w_proj, L1_conv_bn_gamma, L1_conv_bn_beta, L1_conv_bn_mean, L1_conv_bn_var):
    import jax
    import jax.numpy as jnp

    def _L0_conv_ref(fmap, g_norm, q_w1, q_dw, k_w1, k_dw, v_w1, v_dw, out_w, g_out):
        import jax, jax.numpy as jnp
        import numpy as np
        B, DIM, H, W = (16, 128, 16, 16)
        HEADS, DH = (8, 16)
        INNER = HEADS * DH
        EPS = 1e-05

        def chan_ln(x, g):
            mean = jnp.mean(x, axis=1, keepdims=True)
            var = jnp.var(x, axis=1, keepdims=True)
            return (x - mean) * jax.lax.rsqrt(var + EPS) * g[None, :, None, None]

        def depthwise3x3(x, w):
            return jax.lax.conv_general_dilated(x, w, window_strides=(1, 1), padding='SAME', feature_group_count=x.shape[1], dimension_numbers=('NCHW', 'OIHW', 'NCHW'))
        scale = DH ** (-0.5)
        x = chan_ln(fmap, g_norm)

        def proj(w1, dw):
            t = jnp.einsum('bcxy,oc->boxy', x, w1)
            return depthwise3x3(t, dw)
        q, k, v = (proj(q_w1, q_dw), proj(k_w1, k_dw), proj(v_w1, v_dw))

        def split_heads(t):
            b = t.shape[0]
            t = t.reshape(b, HEADS, DH, H * W)
            return t.transpose(0, 1, 3, 2).reshape(b * HEADS, H * W, DH)
        q, k, v = map(split_heads, (q, k, v))
        q = jax.nn.softmax(q, axis=-1) * scale
        k = jax.nn.softmax(k, axis=-2)
        ctx = jnp.einsum('bnd,bne->bde', k, v)
        out = jnp.einsum('bnd,bde->bne', q, ctx)
        out = out.reshape(B, HEADS, H * W, DH).transpose(0, 1, 3, 2)
        out = out.reshape(B, INNER, H, W)
        out = jax.nn.silu(out)
        out = jnp.einsum('bcxy,oc->boxy', out, out_w)
        return chan_ln(out, g_out)

    def _L1_conv_ref(x, w_qkv, w_dw, w_pw, w_proj, bn_gamma, bn_beta, bn_mean, bn_var):
        import jax, jax.numpy as jnp
        from jax import lax
        import numpy as np
        DIM = 8
        BN_EPS = 1e-05
        ATT_EPS = 1e-15
        B, C, H, W = x.shape
        dn = ('NCHW', 'OIHW', 'NCHW')
        qkv = jnp.einsum('bchw,oc->bohw', x, w_qkv)
        y = lax.conv_general_dilated(qkv, w_dw, (1, 1), [(2, 2), (2, 2)], feature_group_count=w_dw.shape[0], dimension_numbers=dn)
        y = lax.conv_general_dilated(y, w_pw, (1, 1), [(0, 0), (0, 0)], feature_group_count=w_pw.shape[0] // w_pw.shape[1], dimension_numbers=dn)
        mqkv = jnp.concatenate([qkv, y], axis=1)
        N = H * W
        mqkv = mqkv.reshape(B, -1, 3 * DIM, N)
        q = jax.nn.relu(mqkv[:, :, :DIM])
        k = jax.nn.relu(mqkv[:, :, DIM:2 * DIM])
        v = mqkv[:, :, 2 * DIM:]
        v = jnp.pad(v, ((0, 0), (0, 0), (0, 1), (0, 0)), constant_values=1.0)
        vk = jnp.einsum('bhdn,bhen->bhde', v, k)
        out = jnp.einsum('bhde,bhen->bhdn', vk, q)
        out = out[:, :, :-1] / (out[:, :, -1:] + ATT_EPS)
        out = out.reshape(B, -1, H, W)
        out = jnp.einsum('bchw,oc->bohw', out, w_proj)
        inv = bn_gamma / jnp.sqrt(bn_var + BN_EPS)
        out = out * inv[None, :, None, None] + (bn_beta - bn_mean * inv)[None, :, None, None]
        return out

    def _gn(v, G=32, eps=1e-05):
        B_, C_, H_, W_ = v.shape
        g = v.reshape(B_, G, C_ // G, H_, W_)
        m = jnp.mean(g, axis=(2, 3, 4), keepdims=True)
        s = jnp.var(g, axis=(2, 3, 4), keepdims=True)
        return ((g - m) / jnp.sqrt(s + eps)).reshape(v.shape)

    def _ln_c(v, eps=1e-06):
        m = jnp.mean(v, axis=1, keepdims=True)
        s = jnp.var(v, axis=1, keepdims=True)
        return (v - m) / jnp.sqrt(s + eps)

    def _ln_t(v, eps=1e-05):
        m = jnp.mean(v, axis=-1, keepdims=True)
        s = jnp.var(v, axis=-1, keepdims=True)
        return (v - m) / jnp.sqrt(s + eps)

    def _to_tokens(v):
        B_, C_, H_, W_ = v.shape
        return v.reshape(B_, C_, H_ * W_).transpose(0, 2, 1)

    def _from_tokens(t, like):
        B_, C_, H_, W_ = like.shape
        return t.transpose(0, 2, 1).reshape(B_, C_, H_, W_)
    x = x + _L0_conv_ref(_gn(x), L0_conv_g_norm, L0_conv_q_w1, L0_conv_q_dw, L0_conv_k_w1, L0_conv_k_dw, L0_conv_v_w1, L0_conv_v_dw, L0_conv_out_w, L0_conv_g_out)
    x = x + _L1_conv_ref(_gn(x), L1_conv_w_qkv, L1_conv_w_dw, L1_conv_w_pw, L1_conv_w_proj, L1_conv_bn_gamma, L1_conv_bn_beta, L1_conv_bn_mean, L1_conv_bn_var)
    return x

_drawn_inputs = setup_inputs


def setup_inputs(seed=0):
    import zlib

    import numpy as np

    out = dict(_drawn_inputs(seed))
    spreads = {'L0_conv_g_norm': (1.0, 0.6),
     'L0_conv_g_out': (1.0, 0.6),
     'L1_conv_bn_gamma': (1.0, 0.6),
     'L1_conv_bn_beta': (0.0, 0.338),
     'L1_conv_bn_mean': (0.0, 0.1),
     'L1_conv_bn_var': (1.0, 0.6)}
    factors = {'L0_conv_q_w1': 8.0,
     'L0_conv_q_dw': 8.0,
     'L0_conv_k_w1': 8.0,
     'L0_conv_k_dw': 8.0,
     'L1_conv_w_qkv': 7.312,
     'L1_conv_w_dw': 8.0,
     'L1_conv_w_pw': 8.0,
     'L1_conv_w_proj': 7.686}
    for name, (base, spread) in spreads.items():
        noise = np.random.default_rng([zlib.crc32(name.encode()), seed]).standard_normal(out[name].shape)
        drawn = base * np.exp(spread * noise) if base else spread * noise
        out[name] = jnp.asarray(drawn.astype(out[name].dtype))
    for name, factor in factors.items():
        out[name] = (out[name] * factor).astype(out[name].dtype)
    return out
```

```python
from contextlib import ExitStack

import concourse.bass as bass
from concourse import mybir

F32 = mybir.dt.float32
I32 = mybir.dt.int32
ALU = mybir.AluOpType
ACT = mybir.ActivationFunctionType
AX = mybir.AxisListType

P = 128
C = 128
B, HH, WW = 16, 16, 16
NPOS = HH * WW
PAIRS = B // 2
PC = 2 * NPOS
XL, XH = 4, 4
CG = 8
NG = 3 * C // CG
GT = C // CG
HD0 = 16
HD1 = 8
NH1 = C // HD1
K0, K1 = 3, 5
PITCH0 = WW + K0 // 2
PITCH1 = WW + K1 // 2
PAD = 16
TSLOTS = 4
EPS = 1e-5
ATT_EPS = 1e-15
RSQRT_MAGIC = 1597463007.0
NEWTON = 4
NEWTON = 4
NEWTON = 4
NEWTON = 4






def conv_blocks_kernel(nc, x, g_norm, q_w1, q_dw, k_w1, k_dw, v_w1, v_dw, out_w, g_out,
                       w_qkv, w_dw, w_pw, w_proj, bn_gamma, bn_beta, bn_mean, bn_var, out):
    ctx = ExitStack()
    with ctx:
        def sb(name, shape, dt=F32):
            return ctx.enter_context(nc.sbuf_tensor(name, shape, dt))

        def sem(name):
            return ctx.enter_context(nc.semaphore(name))

        xin = sb("xin", [P, B * NPOS])
        half0 = xin[:, :].rearrange("p (i n) -> p i n", i=PAIRS)
        xres = sb("xres", [P, PAIRS, PC])
        cin = sb("cin", [P, NG, B * HH])
        cpos = sb("cpos", [P, 3, PAIRS, XL, C])
        tband = sb("tband", [P, TSLOTS, K1 * C])
        taps0 = sb("taps0", [P, NG * K0 * PITCH0])
        taps1 = sb("taps1", [P, NG * K1 * PITCH1])
        ring_a = sb("ring_a", [P, 2, PC])
        ring_b = sb("ring_b", [P, 2, PC])
        ring_c = sb("ring_c", [P, 2, PC])
        ring_d = sb("ring_d", [P, 2, PC])
        ring_e = sb("ring_e", [P, 2, PC])
        ring_v = sb("ring_v", [P, 2, 2, XL, C + 1])
        ctxm = sb("ctxm", [P, 2, 2, C + NH1])
        zflat = cpos[0:CG].rearrange("p t i x c -> p (t i x c)")
        Z1 = 4096
        zrow0 = zflat[:, 0:2 * PAD + NG * K0 * PITCH0]
        zrow1 = zflat[:, Z1:Z1 + 2 * PAD + NG * K1 * PITCH1]
        w0t = sb("w0t", [P, 3 * C])
        owt = sb("owt", [P, C])
        w1t = sb("w1t", [P, 3 * C])
        wpt = sb("wpt", [P, 2, C])
        pw = sb("pw", [P, NG, CG])
        ident = sb("ident", [P, P])
        mean4 = sb("mean4", [P, P])
        mask16 = sb("mask16", [P, P])
        mask8 = sb("mask8", [P, P])
        mask_c = sb("mask_c", [P, CG])
        mask_b = sb("mask_b", [P, 2])
        vecs = sb("vecs", [P, 6])
        bn_inv = sb("bn_inv", [P, 1])
        bn_bias = sb("bn_bias", [P, 1])
        gstats = sb("gstats", [P, B, 6])
        gmv = sb("gmv", [P, B, 2])
        gtmp = sb("gtmp", [P, 3, B])
        newt = sb("newt", [P, 3, B])
        gn_s = sb("gn_s", [P, B])
        gn_b = sb("gn_b", [P, B])
        lstats = sb("lstats", [P, XL, 6])
        lmv = sb("lmv", [P, XL, 2])
        ln_s = sb("ln_s", [P, 2, XL])
        ln_b = sb("ln_b", [P, 2, XL])
        kneg = sb("kneg", [P, B])
        ksum = sb("ksum", [P, B])
        krec = sb("krec", [P, B])
        qmax = sb("qmax", [P, PAIRS * XL])
        qsum = sb("qsum", [P, PAIRS * XL])
        den = sb("den", [P, 2, 2, 2, NH1])
        cflat = cin[:, :, :].rearrange("p g n -> p (g n)")
        wst = [cflat[:, n * C:(n + 1) * C] for n in range(9)]
        pwst = cflat[:, 9 * C:9 * C + 3 * CG].rearrange("p (t c) -> p t c", t=3)
        pwrep = cflat[:, 10 * C:13 * C].rearrange("p (t x c) -> p t x c", t=3, x=WW)
        dwst0 = cflat[0:CG, 2048:2048 + NG * K0 * K0]
        dwst1 = cflat[0:CG, 3072:3072 + NG * K1 * K1]

        bank = [ctx.enter_context(nc.psum_tensor(f"bank{n}", [P, 512], F32)) for n in range(8)]

        s_x = sem("x_loaded")
        s_w = sem("weights_loaded")
        s_dw = sem("taps_loaded")
        s_zero = sem("tap_rows_zeroed")
        s_z0 = sem("tap_rows0_ready")
        s_z1 = sem("tap_rows1_ready")
        s_t0 = sem("taps0_shifted")
        s_t1 = sem("taps1_shifted")
        s_pool = sem("pool_chain")
        s_const = sem("constants_ready")
        s_mask = sem("small_masks_ready")
        s_bnw = sem("bn_folded")
        s_wt = sem("weights_transposed")
        s_wte = sem("weights_out_of_psum")
        s_chain = sem("dve_chain")
        s_gnv = sem("gn_operand_ready")
        s_gnp = sem("gn_product_done")
        s_gn = sem("gn_ready")
        s_xp = sem("residual_ready")
        s_xg = sem("a_xg_ready")
        s_xgt = sem("a_xg_transposed")
        s_nrm_t = sem("a_normed_transposed")
        s_xn = sem("a_xn_ready")
        s_ln = sem("ln_ready")
        s_nrm = sem("normed_ready")
        s_qkv = sem("qkv_unit_done")
        s_cin = sem("conv_in_unit_ready")
        s_tb = sem("band_ready")
        s_grp = sem("conv_groups_done")
        s_ce = sem("conv_banks_free")
        s_qs = sem("a_q_shifted")
        s_qe = sem("a_q_exp")
        s_qn = sem("a_q_normed")
        s_kq = sem("a_kq_transposed")
        s_kn = sem("a_k_max_ready")
        s_ke = sem("a_k_exp_ready")
        s_qc = sem("a_q_channel_major")
        s_kt = sem("a_k_back_transposed")
        s_kp = sem("a_k_pos_major")
        s_vm = sem("a_v_masked")
        s_cx = sem("a_ctx_done")
        s_cm = sem("a_ctx_masked")
        s_o = sem("a_attn_done")
        s_th = sem("a_tanh_ready")
        s_sl = sem("a_silu_ready")
        s_pr = sem("a_proj_done")
        s_zt = sem("a_z_transposed")
        s_x1 = sem("x1_ready")
        s_xg1 = sem("b_xg_ready")
        s_q1 = sem("b_q_ready")
        s_k1 = sem("b_k_ready")
        s_v1 = sem("b_v_ready")
        s_kv = sem("b_kv_done")
        s_kvm = sem("b_kv_masked")
        s_qt1 = sem("b_q_transposed")
        s_qc1 = sem("b_q_channel_major")
        s_num = sem("b_attn_done")
        s_div = sem("b_attn_divided")
        s_ot = sem("b_attn_transposed")
        s_half = sem("b_attn_channel_major")
        s_fin = sem("b_proj_done")
        s_y = sem("y_ready")
        s_yp = sem("y_natural")
        s_out = [sem(f"out_stored_{n}") for n in ("even", "odd")]

        block = ctx.enter_context(nc.Block())

        def tile(t, xl):
            return t[:, xl * P:(xl + 1) * P]

        def image(t, b):
            return t.rearrange("p (n b y) -> p n b y", b=2, y=HH)[:, :, b, :]

        def image3(t, b):
            return t.rearrange("p (l h b y) -> p l h b y", l=XL, h=XH, b=2)[:, :, :, b, :]

        def natural(t):
            return t.rearrange("p (y h l) -> p l h y", h=XH, l=XL)

        def head_q(h):
            return cpos[:, 0, :, :, h * HD0:(h + 1) * HD0].rearrange("p i x d -> p (i x) d")

        @block.sync
        def _(sp):
            for n in range(4):
                sp.dma_start(xin[:, n * 1024:(n + 1) * 1024].rearrange("p (b n) -> p b n", b=4),
                             x[4 * n:4 * n + 4].rearrange("b c h w -> c b (h w)")).then_inc(s_x, 16)
            for zrow, taps, ks, ready, done in ((zrow0, taps0, K0, s_z0, s_t0), (zrow1, taps1, K1, s_z1, s_t1)):
                sp.wait_ge(ready, 1)
                for xi in range(WW):
                    o = PAD + ks // 2 - xi
                    sp.dma_start(taps[CG * xi:CG * (xi + 1), :],
                                 zrow[:, o:o + taps.shape[1]]).then_inc(done, 16)
            for i in range(PAIRS):
                sp.wait_ge(s_yp, i + 1)
                sp.dma_start(out[2 * i:2 * i + 2].rearrange("b c h w -> c b (h w)"),
                             ring_b[:, i % 2, :].rearrange("p (b n) -> p b n", b=2)).then_inc(s_out[i % 2], 16)
            for n in range(2):
                sp.wait_ge(s_out[n], 16 * PAIRS // 2)

        @block.gpsimd
        def _(pool):
            g = nc.gpsimd
            links = [0]

            def link(ins):
                links[0] += 1
                ins.then_inc(s_pool, 1)
                pool.wait_ge(s_pool, links[0])

            g.memset(zrow0, 0.0)
            g.memset(zrow1, 0.0).then_inc(s_zero, 1)
            g.memset(mean4[:, :], 1.0 / 4)
            g.memset(mask16[:, :], float(HD0) ** -0.5)
            g.memset(mask8[:, :], 1.0)
            link(g.memset(ident[:, :], 0.0))
            g.affine_select(out=ident[:, :], in_=ident[:, :], compare_op=ALU.not_equal, fill=1.0,
                            base=0, pattern=[[-1, P]], channel_multiplier=1)
            for base, sign in ((0, 1), (1, -1)):
                for m, w in ((mean4, 4), (mask16, HD0), (mask8, HD1)):
                    mw = m[:, :].rearrange("p (n w) -> p n w", w=w)
                    last = g.affine_select(out=mw, in_=mw, compare_op=ALU.is_ge, fill=0.0,
                                           base=base * (w - 1), pattern=[[-sign * w, P // w], [0, w]],
                                           channel_multiplier=sign)
                link(last)
            pool.sem_inc(s_const, 1)

            pool.wait_ge(s_x, 16 * 4)
            for b in range(B):
                g.tensor_copy(image3(xres[:, b // 2, :], b % 2),
                              natural(xin[:, b * NPOS:(b + 1) * NPOS])).then_inc(s_xp, 1)

            pool.wait_ge(s_t0, 16 * WW)
            pool.wait_ge(s_mask, 1)
            d0 = taps0[:, :].rearrange("p (g k n) -> p g k n", g=NG, k=K0)
            with pool.Fori(0, NG // TSLOTS) as it:
                for j in range(TSLOTS):
                    pool.wait_ge(s_grp, it * TSLOTS + (j + 1))
                    src = d0[:, bass.ds(it * TSLOTS + j, 1), :, 0:WW].rearrange("p g k n -> p (g k) n")
                    g.tensor_tensor(out=tband[:, j, 0:K0 * C].rearrange("p (k x o) -> p k x o", k=K0, o=CG),
                                    in0=src.unsqueeze(3).broadcast_to([P, K0, WW, CG]),
                                    in1=mask_c[:, :].unsqueeze(1).unsqueeze(1).broadcast_to([P, K0, WW, CG]),
                                    op=ALU.mult).then_inc(s_tb, 1)

            def mask_v(i, ready):
                for b in range(2):
                    last = g.tensor_scalar(ring_v[:, i % 2, b, :, 0:C], cpos[:, 2, i], mask_b[:, b:b + 1], 1.0,
                                           ALU.mult, ALU.mult)
                last.then_inc(ready, 1)

            pool.wait_ge(s_ce, 2 + NG // 2)
            for i in range(PAIRS):
                if i >= 2:
                    pool.wait_ge(s_cx, i - 1)
                mask_v(i, s_vm)

            pool.wait_ge(s_t1, 16 * WW)
            pool.wait_ge(s_wte, 1)
            d1 = taps1[:, :].rearrange("p (h t k n) -> p h t k n", t=3, k=K1, n=PITCH1)
            pwv = pw[:, :, :].rearrange("p (h t) o -> p h t o", t=3)
            for t in range(3):
                with pool.Fori(0, GT // TSLOTS) as it:
                    for j in range(TSLOTS):
                        pool.wait_ge(s_grp, it * TSLOTS + (NG + t * GT + j + 1))
                        src = d1[:, bass.ds(it * TSLOTS + j, 1), t, :, 0:WW].rearrange("p h k n -> p (h k) n")
                        w = pwv[:, bass.ds(it * TSLOTS + j, 1), t, :]
                        g.tensor_tensor(out=tband[:, j, :].rearrange("p (k x o) -> p k x o", k=K1, o=CG),
                                        in0=src.unsqueeze(3).broadcast_to([P, K1, WW, CG]),
                                        in1=w.unsqueeze(1).broadcast_to([P, K1, WW, CG]),
                                        op=ALU.mult).then_inc(s_tb, 1)

            pool.wait_ge(s_ce, 2 + NG)
            for i in range(PAIRS):
                pool.wait_ge(s_kv, PAIRS + i - 1)
                mask_v(i, s_v1)

        @block.scalar
        def _(act):
            a = nc.scalar
            for n, w in enumerate((q_w1, k_w1, v_w1, out_w)):
                act.dma_start(wst[n], w).then_inc(s_w, 16)
            act.dma_start(cflat[:, 4 * C:7 * C].rearrange("p (t c) -> p t c", t=3),
                          w_qkv.rearrange("(t p) c -> p t c", t=3)).then_inc(s_w, 16)
            act.dma_start(cflat[:, 7 * C:9 * C], w_proj).then_inc(s_w, 16)
            act.dma_start(pwst, w_pw.rearrange("(t p) c h w -> p t (c h w)", t=3)).then_inc(s_w, 16)
            for n, vec in enumerate((g_norm, g_out, bn_gamma, bn_beta, bn_mean, bn_var)):
                act.dma_start(vecs[:, n:n + 1], vec.rearrange("(c a) -> c a", a=1)).then_inc(s_w, 16)
            for t, w in enumerate((q_dw, k_dw, v_dw)):
                n = GT * K0 * K0
                act.dma_start(dwst0[:, t * n:(t + 1) * n].rearrange("c (g k) -> c g k", g=GT),
                              w.rearrange("(g c) a h w -> c g (a h w)", c=CG)).then_inc(s_dw, 16)
            act.dma_start(dwst1.rearrange("c (g k) -> c g k", g=NG),
                          w_dw.rearrange("(g c) a h w -> c g (a h w)", c=CG)).then_inc(s_dw, 16)

            act.wait_ge(s_wt, 1)
            a.activation(w0t[:, :], bank[0][:, 0:3 * C], ACT.Copy, scale=vecs[:, 0:1])
            a.mul(owt[:, :], bank[0][:, 3 * C:4 * C], 0.5)
            a.copy(w1t[:, :], bank[1][:, 0:3 * C])
            a.copy(pw[:, :, :].rearrange("p g c -> p (g c)"), bank[2][:, 0:3 * C])
            a.copy(wpt[:, :, :].rearrange("p t c -> p (t c)"), bank[3][:, 0:2 * C]).then_inc(s_wte, 1)

            def normed(n, src, dst):
                act.wait_ge(s_ln, n + 1)
                for xl in range(XL):
                    last = a.activation(tile(dst, xl), tile(src, xl), ACT.Identity,
                                        scale=ln_s[:, n % 2, xl:xl + 1], bias=ln_b[:, n % 2, xl:xl + 1])
                last.then_inc(s_nrm, 1)

            def xg(i):
                if i >= 2:
                    act.wait_ge(s_xgt, i - 1)
                for b in range(2):
                    n = 2 * i + b
                    last = a.activation(image3(ring_a[:, i % 2, :], b), natural(xin[:, n * NPOS:(n + 1) * NPOS]),
                                        ACT.Identity, scale=gn_s[:, n:n + 1], bias=gn_b[:, n:n + 1])
                last.then_inc(s_xg, 1)

            def front_normed(i):
                if i >= 2:
                    act.wait_ge(s_nrm_t, i - 1)
                normed(i, bank[i % 2][:, :], ring_b[:, i % 2, :])

            def xn(i):
                act.wait_ge(s_nrm_t, i + 1)
                if i >= 2:
                    act.wait_ge(s_qkv, 3 * (i - 1))
                a.copy(ring_c[:, i % 2, :], bank[2 + i % 2][:, :]).then_inc(s_xn, 1)

            act.wait_ge(s_gn, 1)
            for step in range(PAIRS + 2):
                if step < PAIRS:
                    xg(step)
                if 0 <= step - 1 < PAIRS:
                    front_normed(step - 1)
                if 0 <= step - 2 < PAIRS:
                    xn(step - 2)

            for h in range(C // HD0):
                act.wait_ge(s_qs, h + 1)
                a.activation(head_q(h), head_q(h), ACT.Exp).then_inc(s_qe, 1)

            def k_exp(i):
                act.wait_ge(s_kn, i + 1)
                if i >= 2:
                    act.wait_ge(s_kt, i - 1)
                for b in range(2):
                    n = 2 * i + b
                    last = a.activation(image(ring_a[:, i % 2, :], b), image(bank[0][:, :], b), ACT.Exp,
                                        bias=kneg[:, n:n + 1], accum_out=ksum[:, n:n + 1])
                last.then_inc(s_ke, 1)

            def q_out(i):
                if i >= 2:
                    act.wait_ge(s_o, i - 1)
                a.copy(ring_b[:, i % 2, :], bank[1][:, :]).then_inc(s_qc, 1)

            def k_out(i):
                act.wait_ge(s_kt, i + 1)
                if i >= 2:
                    act.wait_ge(s_cx, i - 1)
                a.copy(ring_c[:, i % 2, :], bank[2][:, :]).then_inc(s_kp, 1)

            def tanh(i):
                act.wait_ge(s_o, i + 1)
                if i >= 2:
                    act.wait_ge(s_pr, i - 1)
                a.activation(ring_d[:, i % 2, :], bank[4][:, :], ACT.Tanh, scale=0.5).then_inc(s_th, 1)

            def z_normed(i):
                if i >= 2:
                    act.wait_ge(s_zt, i - 1)
                normed(PAIRS + i, bank[5][:, :], ring_e[:, i % 2, :])

            for step in range(PAIRS + 4):
                if 0 <= step - 4 < PAIRS:
                    z_normed(step - 4)
                if 0 <= step - 3 < PAIRS:
                    tanh(step - 3)
                if 0 <= step - 1 < PAIRS:
                    k_out(step - 1)
                if step < PAIRS:
                    k_exp(step)
                    q_out(step)

            def xg1(i):
                act.wait_ge(s_gn, 2 + i // (PAIRS // 2))
                act.wait_ge(s_kt, PAIRS) if i < 2 else act.wait_ge(s_qkv, 3 * PAIRS + 3 * (i - 1))
                for b in range(2):
                    n = 2 * i + b
                    last = a.activation(image(ring_a[:, i % 2, :], b), image(xres[:, i, :], b),
                                        ACT.Identity, scale=gn_s[:, n:n + 1], bias=gn_b[:, n:n + 1])
                last.then_inc(s_xg1, 1)

            def front1(i):
                act.wait_ge(s_cin, 3 * PAIRS + 3 * i + 1)
                act.wait_ge(s_o, PAIRS) if i < 2 else act.wait_ge(s_qt1, i - 1)
                a.activation(ring_b[:, i % 2, :], bank[0][:, :], ACT.Relu).then_inc(s_q1, 1)
                act.wait_ge(s_cin, 3 * PAIRS + 3 * i + 2)
                act.wait_ge(s_cx, PAIRS) if i < 2 else act.wait_ge(s_kv, i - 1)
                a.activation(ring_c[:, i % 2, :], bank[1][:, :], ACT.Relu).then_inc(s_k1, 1)
                act.wait_ge(s_cin, 3 * PAIRS + 3 * i + 3)
                for b in range(2):
                    last = a.activation(ring_v[:, i % 2, b, :, 0:C],
                                        bank[2][:, :].rearrange("p (x c) -> p x c", x=XL),
                                        ACT.Copy, scale=mask_b[:, b:b + 1])
                last.then_inc(s_v1, 1)

            def q_out1(n):
                act.wait_ge(s_qt1, n + 1)
                act.wait_ge(s_pr, PAIRS) if n < 2 else act.wait_ge(s_num, n - 1)
                a.activation(ring_d[:, n % 2, :].rearrange("p (b n y) -> p n b y", b=2, y=HH),
                             bank[3][:, :].rearrange("p (n b y) -> p n b y", b=2, y=HH),
                             ACT.Copy if n < PAIRS else ACT.Relu).then_inc(s_qc1, 1)

            def half_out(i):
                act.wait_ge(s_ot, i + 1)
                a.copy(half0[:, i, :], bank[7][:, :]).then_inc(s_half, 1)

            for step in range(PAIRS + 4):
                if 0 <= step - 3 < PAIRS:
                    half_out(step - 3)
                if 0 <= step - 1 < PAIRS:
                    q_out1(step - 1)
                if step < PAIRS:
                    xg1(step)
                    front1(step)

            def k_relu(i):
                act.wait_ge(s_kv, PAIRS + i - 1)
                a.activation(ring_c[:, i % 2, :], cpos[:, 1, i].rearrange("p x c -> p (x c)"),
                             ACT.Relu).then_inc(s_k1, 1)

            def half1_out(i):
                act.wait_ge(s_ot, PAIRS + i + 1)
                if i >= 2:
                    act.wait_ge(s_fin, i - 1)
                a.copy(ring_a[:, i % 2, :], bank[7][:, :]).then_inc(s_half, 1)

            def y_out(i):
                act.wait_ge(s_y, i + 1)
                if i >= 2:
                    act.wait_ge(s_out[i % 2], 16 * (i // 2))
                for b in range(2):
                    last = a.copy(natural(ring_b[:, i % 2, b * NPOS:(b + 1) * NPOS]), image3(xres[:, i, :], b))
                last.then_inc(s_yp, 1)

            act.wait_ge(s_ce, 2 + NG)
            for step in range(PAIRS + 4):
                if 0 <= step - 4 < PAIRS:
                    y_out(step - 4)
                if 0 <= step - 2 < PAIRS:
                    half1_out(step - 2)
                if step < PAIRS:
                    k_relu(step)
                    q_out1(PAIRS + step)

        @block.vector
        def _(dve):
            v = nc.vector
            links = [0]

            def link(ins):
                links[0] += 1
                ins.then_inc(s_chain, 1)
                dve.wait_ge(s_chain, links[0])

            def rsqrt(dst, var, n):
                w, y, t = newt[:, 0, 0:n], newt[:, 1, 0:n], newt[:, 2, 0:n]
                link(v.tensor_scalar(w, var, EPS, None, ALU.add))
                link(v.tensor_scalar(y.bitcast(I32), w.bitcast(I32), -0.5, RSQRT_MAGIC, ALU.mult, ALU.add))
                for k in range(NEWTON):
                    link(v.tensor_tensor(t, y, y, ALU.mult))
                    link(v.scalar_tensor_tensor(out=t, in0=t, scalar=-0.5, in1=w, op0=ALU.mult, op1=ALU.mult))
                    link(v.scalar_tensor_tensor(out=y if k < NEWTON - 1 else dst, in0=t, scalar=1.5, in1=y,
                                                op0=ALU.add, op1=ALU.mult))

            dve.wait_ge(s_zero, 1)
            dve.wait_ge(s_dw, 16 * 4)
            for zrow, st, ks, pitch, ready in ((zrow0, dwst0, K0, PITCH0, s_z0), (zrow1, dwst1, K1, PITCH1, s_z1)):
                rows = zrow[:, PAD:PAD + NG * ks * pitch].rearrange("c (r n) -> c r n", n=pitch)
                v.tensor_copy(rows[:, :, 0:ks], st.rearrange("c (r k) -> c r k", k=ks)[:, :, ::-1]).then_inc(ready, 1)

            dve.wait_ge(s_const, 1)
            v.tensor_reduce(mask_c[:, :], ident[:, :].rearrange("p (j o) -> p o j", o=CG), op=ALU.add, axis=AX.X)
            link(v.tensor_reduce(mask_b[:, :], ident[:, :].rearrange("p (h b y) -> p b h y", h=XH, b=2),
                                 op=ALU.add, axis=AX.XY))
            for s in range(2):
                for xl in range(XL):
                    last = v.tensor_copy(ring_v[:, s, :, xl, C], mask_b[:, :])
            last.then_inc(s_mask, 1)

            dve.wait_ge(s_w, 16 * 13)
            for t in range(3):
                v.tensor_copy(pwrep[:, t], pwst[:, t, :].unsqueeze(1).broadcast_to([P, WW, CG]))
            rsqrt(bn_inv[:, :], vecs[:, 5:6], 1)
            link(v.tensor_tensor(bn_bias[:, :], bn_inv[:, :], vecs[:, 2:3], ALU.mult))
            v.tensor_scalar(cflat[:, 7 * C:9 * C], cflat[:, 7 * C:9 * C], bn_bias[:, :], None, ALU.mult).then_inc(s_bnw, 1)
            link(v.tensor_tensor(bn_inv[:, :], bn_bias[:, :], vecs[:, 4:5], ALU.mult))
            v.tensor_tensor(bn_bias[:, :], vecs[:, 3:4], bn_inv[:, :], ALU.subtract)

            def gn_aggregate(c, b0, n):
                for b in range(b0, b0 + n):
                    last = v.bn_aggr(gmv[:, b, :], gstats[:, b, :])
                last.then_inc(s_gnv, 1)

            def gn_variance(c, b0, n, ps):
                m, d = gtmp[:, 0, 0:n], gtmp[:, 1, 0:n]
                dve.wait_ge(s_gnp, 2 * c + 1)
                dve.wait_ge(s_gnv, 2 * c + 1)
                link(v.tensor_copy(m, ps[:, 0:n]))
                link(v.tensor_tensor(d, gmv[:, b0:b0 + n, 0], m, ALU.subtract))
                link(v.tensor_tensor(d, d, d, ALU.mult))
                v.tensor_tensor(gmv[:, b0:b0 + n, 1], gmv[:, b0:b0 + n, 1], d, ALU.add).then_inc(s_gnv, 1)

            def gn_scale(c, b0, n, ps):
                dve.wait_ge(s_gnp, 2 * c + 2)
                link(v.tensor_copy(gtmp[:, 2, 0:n], ps[:, B:B + n]))
                rsqrt(gn_s[:, b0:b0 + n], gtmp[:, 2, 0:n], n)
                v.scalar_tensor_tensor(out=gn_b[:, b0:b0 + n], in0=gtmp[:, 0, 0:n], scalar=-1.0,
                                       in1=gn_s[:, b0:b0 + n], op0=ALU.mult, op1=ALU.mult).then_inc(s_gn, 1)

            def layernorm(n, src):
                for xl in range(XL):
                    last = v.bn_stats(lstats[:, xl, :], tile(src, xl))
                link(last)
                for xl in range(XL):
                    last = v.bn_aggr(lmv[:, xl, :], lstats[:, xl, :])
                link(last)
                if n >= 2:
                    dve.wait_ge(s_nrm, n - 1)
                rsqrt(ln_s[:, n % 2, :], lmv[:, :, 1], XL)
                v.scalar_tensor_tensor(out=ln_b[:, n % 2, :], in0=lmv[:, :, 0], scalar=-1.0,
                                       in1=ln_s[:, n % 2, :], op0=ALU.mult, op1=ALU.mult).then_inc(s_ln, 1)

            def conv_in(t, i, ps):
                v.transpose(cin[:, t * GT:(t + 1) * GT, 32 * i:32 * i + 32],
                            ps[:, :].rearrange("p (x g c) -> p g x c", x=XL, c=CG)).then_inc(s_cin, 1)

            for b in range(B):
                if b % 4 == 0:
                    dve.wait_ge(s_x, 64)
                last = v.bn_stats(gstats[:, b, :], xin[:, b * NPOS:(b + 1) * NPOS])
            link(last)
            gn_aggregate(0, 0, B)
            gn_variance(0, 0, B, bank[7])
            gn_scale(0, 0, B, bank[7])
            for step in range(PAIRS + 3):
                if 0 <= step - 3 < PAIRS:
                    for t in range(3):
                        u = 3 * (step - 3) + t
                        dve.wait_ge(s_qkv, u + 1)
                        conv_in(t, step - 3, bank[4 + u % 4])
                if step < PAIRS:
                    dve.wait_ge(s_xgt, step + 1)
                    layernorm(step, bank[step % 2][:, :])

            def conv_out(n):
                dve.wait_ge(s_grp, TSLOTS + 2 * (n + 1))
                for j in range(2):
                    t, g = divmod((2 * n + j) % NG, GT)
                    last = v.transpose(cpos[:, t, :, :, g * CG:(g + 1) * CG],
                                       bank[n % 2][:, j * B * HH:(j + 1) * B * HH])
                last.then_inc(s_ce, 1)

            def over_head(t):
                return t[:, :].unsqueeze(2).broadcast_to([P, PAIRS * XL, HD0])

            def q_shift(h):
                dve.wait_ge(s_ce, 2 + h + 1)
                if h:
                    dve.wait_ge(s_qs, h)
                link(v.tensor_reduce(qmax[:, :], head_q(h), op=ALU.max, axis=AX.X))
                v.tensor_tensor(head_q(h), head_q(h), over_head(qmax), ALU.subtract).then_inc(s_qs, 1)

            def q_scale(h):
                dve.wait_ge(s_qe, h + 1)
                if h:
                    dve.wait_ge(s_qn, h)
                link(v.tensor_reduce(qsum[:, :], head_q(h), op=ALU.add, axis=AX.X))
                link(v.reciprocal(qsum[:, :], qsum[:, :]))
                v.tensor_tensor(head_q(h), head_q(h), over_head(qsum), ALU.mult).then_inc(s_qn, 1)

            dve.wait_ge(s_t0, 16 * WW)
            dve.wait_ge(s_t1, 16 * WW)
            heads = C // HD0
            for n in range(NG // 2):
                conv_out(n)
                if 1 <= n <= heads:
                    q_shift(n - 1)
                if 3 <= n <= heads + 2:
                    q_scale(n - 3)

            def k_max(i):
                dve.wait_ge(s_kq, i + 1)
                v.tensor_reduce(kneg[:, 2 * i:2 * i + 2],
                                bank[0][:, :].rearrange("p (n b y) -> p b n y", b=2, y=HH),
                                op=ALU.max, axis=AX.XY, negate=True).then_inc(s_kn, 1)

            def ctx_mask(i):
                dve.wait_ge(s_ke, i + 1)
                link(v.reciprocal(krec[:, 2 * i:2 * i + 2], ksum[:, 2 * i:2 * i + 2]))
                dve.wait_ge(s_cx, i + 1)
                if i >= 2:
                    dve.wait_ge(s_o, i - 1)
                for b in range(2):
                    last = v.scalar_tensor_tensor(
                        out=ctxm[:, i % 2, b, 0:C], in0=bank[3][:, b * C:(b + 1) * C],
                        scalar=krec[:, 2 * i + b:2 * i + b + 1], in1=mask16[:, :], op0=ALU.mult, op1=ALU.mult)
                last.then_inc(s_cm, 1)

            def silu(i):
                dve.wait_ge(s_th, i + 1)
                v.scalar_tensor_tensor(out=ring_d[:, i % 2, :], in0=ring_d[:, i % 2, :], scalar=1.0,
                                       in1=bank[4][:, :], op0=ALU.add, op1=ALU.mult).then_inc(s_sl, 1)

            def x1(i):
                dve.wait_ge(s_zt, i + 1)
                dve.wait_ge(s_xp, 2 * i + 2)
                v.scalar_tensor_tensor(out=xres[:, i, :], in0=bank[7][:, :], scalar=vecs[:, 1:2],
                                       in1=xres[:, i, :], op0=ALU.mult, op1=ALU.add).then_inc(s_x1, 1)

            def x1_stats(i):
                dve.wait_ge(s_x1, i + 1)
                for b in range(2):
                    last = v.bn_stats(gstats[:, 2 * i + b, :], image(xres[:, i, :], b))
                if i % (PAIRS // 2) == PAIRS // 2 - 1:
                    link(last)
                    gn_aggregate(1 + 2 * i // B, 2 * i + 2 - B // 2, B // 2)

            for step in range(PAIRS + 6):
                if 0 <= step - 6 < PAIRS:
                    x1_stats(step - 6)
                if step == PAIRS // 2 + 6:
                    gn_variance(1, 0, B // 2, bank[6])
                if step == PAIRS // 2 + 7:
                    gn_scale(1, 0, B // 2, bank[6])
                if 0 <= step - 5 < PAIRS:
                    x1(step - 5)
                if 0 <= step - 4 < PAIRS:
                    dve.wait_ge(s_pr, step - 4 + 1)
                    layernorm(PAIRS + step - 4, bank[5][:, :])
                if 0 <= step - 3 < PAIRS:
                    silu(step - 3)
                if 0 <= step - 2 < PAIRS:
                    ctx_mask(step - 2)
                if step < PAIRS:
                    k_max(step)

            def kv_mask(n):
                dve.wait_ge(s_kv, n + 1)
                dve.wait_ge(s_o, PAIRS) if n < 2 else dve.wait_ge(s_num, n - 1)
                for b in range(2):
                    o = b * (C + 1)
                    v.tensor_tensor(ctxm[:, n % 2, b, 0:C], bank[4][:, o:o + C], mask8[:, :], ALU.mult)
                    last = v.tensor_scalar(ctxm[:, n % 2, b, C:C + NH1],
                                           mask8[:, :].rearrange("p (h d) -> p h d", d=HD1)[:, :, 0],
                                           bank[4][:, o + C:o + C + 1], None, ALU.mult)
                last.then_inc(s_kvm, 1)

            def attn_div(n):
                dve.wait_ge(s_num, n + 1)
                dve.wait_ge(s_zt, PAIRS) if n < 2 else dve.wait_ge(s_ot, n - 1)
                s = n % 2
                tiles = [bank[5 + b][:, 0:2 * (C + NH1)].rearrange("p (j c) -> p j c", j=2) for b in range(2)]
                for b in range(2):
                    last = v.tensor_scalar(den[:, s, b, :, :], tiles[b][:, :, C:C + NH1], ATT_EPS, None, ALU.add)
                link(last)
                dv = den[:, s, :, :, :].rearrange("p b j h -> p (b j h)")
                link(v.reciprocal(dv, dv))
                for b in range(2):
                    last = v.tensor_tensor(
                        ring_e[:, s, 2 * b * C:2 * (b + 1) * C].rearrange("p (j h d) -> p j h d", j=2, d=HD1),
                        tiles[b][:, :, 0:C].rearrange("p j (h d) -> p j h d", d=HD1),
                        den[:, s, b, :, :].unsqueeze(3).broadcast_to([P, 2, NH1, HD1]), ALU.mult)
                last.then_inc(s_div, 1)

            for step in range(PAIRS + 3):
                if 0 <= step - 2 < PAIRS:
                    attn_div(step - 2)
                if 0 <= step - 1 < PAIRS:
                    kv_mask(step - 1)
                if step == 0:
                    gn_variance(2, B // 2, B // 2, bank[7])
                if step == 1:
                    gn_scale(2, B // 2, B // 2, bank[7])
                if step < PAIRS:
                    for t in range(3):
                        dve.wait_ge(s_qkv, 3 * PAIRS + 3 * step + t + 1)
                        conv_in(t, step, bank[t])

            for n in range(NG // 2, NG):
                conv_out(n)

            def y(i):
                dve.wait_ge(s_fin, i + 1)
                for b in range(2):
                    r = image(xres[:, i, :], b)
                    last = v.scalar_tensor_tensor(
                        out=r, in0=bank[2][:, b * NPOS:(b + 1) * NPOS].rearrange("p (n y) -> p n y", y=HH),
                        scalar=bn_bias[:, :], in1=r, op0=ALU.add, op1=ALU.add)
                last.then_inc(s_y, 1)

            for step in range(PAIRS + 3):
                if 0 <= step - 3 < PAIRS:
                    y(step - 3)
                if 0 <= step - 1 < PAIRS:
                    attn_div(PAIRS + step - 1)
                if step < PAIRS:
                    kv_mask(PAIRS + step)

        @block.tensor
        def _(pe):
            t_ = nc.tensor

            def transposes(dst, src):
                for xl in range(XL):
                    last = t_.transpose(tile(dst, xl), src(xl), ident[:, :])
                return last

            def product(dst, stationary, moving, start=True, stop=True):
                return t_.matmul(dst, stationary, moving, start=start, stop=stop, skip_group_check=True)

            pe.wait_ge(s_const, 1)
            pe.wait_ge(s_bnw, 1)
            for dst, first, count in ((bank[0], 0, 4), (bank[1], 4, 3), (bank[3], 7, 2)):
                for n in range(count):
                    t_.transpose(tile(dst, n), wst[first + n], ident[:, :])
            for n in range(3):
                last = product(tile(bank[2], n), pwrep[:, n].rearrange("p x c -> p (x c)"), ident[:, :])
            last.then_inc(s_wt, 1)

            def gn_mean(c, k, b0, n, ps):
                pe.wait_ge(s_gnv, 2 * c + k + 1)
                product(ps[:, B * k:B * k + n], mean4[:, :], gmv[:, b0:b0 + n, k]).then_inc(s_gnp, 1)

            gn_mean(0, 0, 0, B, bank[7])
            gn_mean(0, 1, 0, B, bank[7])
            pe.wait_ge(s_wte, 1)
            for step in range(PAIRS + 3):
                if 0 <= step - 3 < PAIRS:
                    i = step - 3
                    pe.wait_ge(s_xn, i + 1)
                    for t in range(3):
                        u = 3 * i + t
                        if u >= 4:
                            pe.wait_ge(s_cin, u - 3)
                        if u == 3:
                            pe.wait_ge(s_gn, 1)
                        for xl in range(XL):
                            last = product(tile(bank[4 + u % 4], xl), tile(ring_c[:, i % 2, :], xl),
                                           w0t[:, t * C:(t + 1) * C])
                        last.then_inc(s_qkv, 1)
                if 0 <= step - 2 < PAIRS:
                    i = step - 2
                    pe.wait_ge(s_nrm, i + 1)
                    if i >= 2:
                        pe.wait_ge(s_xn, i - 1)
                    transposes(bank[2 + i % 2], lambda xl: tile(ring_b[:, i % 2, :], xl)).then_inc(s_nrm_t, 1)
                if step < PAIRS:
                    i = step
                    pe.wait_ge(s_xg, i + 1)
                    if i >= 2:
                        pe.wait_ge(s_nrm, i - 1)
                    transposes(bank[i % 2], lambda xl: tile(ring_a[:, i % 2, :], xl)).then_inc(s_xgt, 1)

            def conv(which, ks):
                order = [ks // 2] + [k for k in range(ks) if k != ks // 2]
                with pe.Fori(0, NG // TSLOTS) as it:
                    for j in range(TSLOTS):
                        dst = bank[j // 2][:, (j % 2) * B * HH:(j % 2 + 1) * B * HH].rearrange("p (b y) -> p b y", b=B)
                        src = cin[:, bass.ds(it * TSLOTS + j, 1), :].rearrange("p g (b y) -> p (g b) y", b=B)
                        if j % 2 == 0:
                            pe.wait_ge(s_ce, it * 2 + (which * (NG // 2) + j // 2 + 1))
                        pe.wait_ge(s_tb, it * TSLOTS + (which * NG + j + 1))
                        for k in order:
                            dy = k - ks // 2
                            lo, hi = max(0, -dy), min(HH, HH - dy)
                            last = product(dst[:, :, lo:hi], tband[:, j, k * C:(k + 1) * C], src[:, :, lo + dy:hi + dy],
                                           start=k == ks // 2, stop=k == order[-1])
                        last.then_inc(s_grp, 1)

            pe.sem_inc(s_grp, TSLOTS)
            pe.sem_inc(s_ce, 2)
            pe.wait_ge(s_nrm, PAIRS)
            pe.wait_ge(s_cin, 3 * PAIRS)
            conv(0, K0)

            def kq_transpose(i):
                if i == 0:
                    pe.wait_ge(s_ce, 2 + NG // 2)
                    pe.wait_ge(s_qn, C // HD0)
                else:
                    pe.wait_ge(s_ke, i)
                    pe.wait_ge(s_qc, i)
                transposes(bank[0], lambda xl: cpos[:, 1, i, xl])
                transposes(bank[1], lambda xl: cpos[:, 0, i, xl]).then_inc(s_kq, 1)

            def k_back(i):
                pe.wait_ge(s_ke, i + 1)
                if i >= 1:
                    pe.wait_ge(s_kp, i)
                transposes(bank[2], lambda xl: tile(ring_a[:, i % 2, :], xl)).then_inc(s_kt, 1)

            def context(i):
                pe.wait_ge(s_kp, i + 1)
                pe.wait_ge(s_vm, i + 1)
                if i >= 1:
                    pe.wait_ge(s_cm, i)
                for xl in range(XL):
                    last = product(bank[3][:, 0:2 * C], tile(ring_c[:, i % 2, :], xl), ring_v[:, i % 2, :, xl, 0:C],
                                   start=xl == 0, stop=xl == XL - 1)
                last.then_inc(s_cx, 1)

            def attend(i):
                pe.wait_ge(s_cm, i + 1)
                pe.wait_ge(s_qc, i + 1)
                if i >= 1:
                    pe.wait_ge(s_sl, i)
                for b in range(2):
                    last = product(image(bank[4][:, :], b), ctxm[:, i % 2, b, 0:C], image(ring_b[:, i % 2, :], b))
                last.then_inc(s_o, 1)

            def project(i):
                pe.wait_ge(s_sl, i + 1)
                if i >= 1:
                    pe.wait_ge(s_nrm, PAIRS + i)
                for xl in range(XL):
                    last = product(tile(bank[5], xl), tile(ring_d[:, i % 2, :], xl), owt[:, :])
                last.then_inc(s_pr, 1)

            def z_transpose(i):
                pe.wait_ge(s_nrm, PAIRS + i + 1)
                if i >= 1:
                    pe.wait_ge(s_x1, i)
                transposes(bank[7], lambda xl: tile(ring_e[:, i % 2, :], xl)).then_inc(s_zt, 1)

            for step in range(PAIRS + 5):
                if step == PAIRS // 2 + 6:
                    gn_mean(1, 0, 0, B // 2, bank[6])
                if step == PAIRS // 2 + 7:
                    gn_mean(1, 1, 0, B // 2, bank[6])
                if 0 <= step - 5 < PAIRS:
                    z_transpose(step - 5)
                if 0 <= step - 4 < PAIRS:
                    project(step - 4)
                if 0 <= step - 3 < PAIRS:
                    attend(step - 3)
                if 0 <= step - 2 < PAIRS:
                    context(step - 2)
                if 0 <= step - 1 < PAIRS:
                    k_back(step - 1)
                if step < PAIRS:
                    kq_transpose(step)

            def qkv1(i):
                pe.wait_ge(s_xg1, i + 1)
                w = w1t[:, :].rearrange("p (h t e) -> p t h e", t=3, e=HD1)
                for t, (free, free0) in enumerate(((s_q1, s_qc), (s_k1, s_kp), (s_v1, s_kp))):
                    if i == 0:
                        pe.wait_ge(s_ke, PAIRS)
                        pe.wait_ge(free0, PAIRS)
                    else:
                        pe.wait_ge(free, i)
                    for xl in range(XL):
                        last = product(tile(bank[t], xl), tile(ring_a[:, i % 2, :], xl), w[:, t])
                    last.then_inc(s_qkv, 1)

            def q_transpose1(n, src):
                if n == 0:
                    pe.wait_ge(s_cm, PAIRS)
                else:
                    pe.wait_ge(s_qc1, n)
                transposes(bank[3], src).then_inc(s_qt1, 1)

            def kv_product(n):
                pe.wait_ge(s_k1, n + 1)
                pe.wait_ge(s_v1, n + 1)
                if n == 0:
                    pe.wait_ge(s_sl, PAIRS)
                else:
                    pe.wait_ge(s_kvm, n)
                for xl in range(XL):
                    last = product(bank[4][:, 0:2 * (C + 1)], tile(ring_c[:, n % 2, :], xl), ring_v[:, n % 2, :, xl, :],
                                   start=xl == 0, stop=xl == XL - 1)
                last.then_inc(s_kv, 1)

            def attend1(n):
                pe.wait_ge(s_kvm, n + 1)
                pe.wait_ge(s_qc1, n + 1)
                if n == 0:
                    pe.wait_ge(s_nrm, 2 * PAIRS)
                    pe.wait_ge(s_gn, 2)
                else:
                    pe.wait_ge(s_div, n)
                for b in range(2):
                    for j in range(2):
                        last = product(bank[5 + b][:, j * (C + NH1):(j + 1) * (C + NH1)],
                                       tile(ring_d[:, n % 2, :], 2 * b + j), ctxm[:, n % 2, b, :])
                last.then_inc(s_num, 1)

            def o_transpose(n):
                pe.wait_ge(s_div, n + 1)
                if n == 0:
                    pe.wait_ge(s_gn, 3)
                else:
                    pe.wait_ge(s_half, n)
                transposes(bank[7], lambda xl: tile(ring_e[:, n % 2, :], xl)).then_inc(s_ot, 1)

            for step in range(PAIRS + 4):
                if 0 <= step - 3 < PAIRS:
                    o_transpose(step - 3)
                if 0 <= step - 2 < PAIRS:
                    attend1(step - 2)
                if 0 <= step - 1 < PAIRS:
                    i = step - 1
                    pe.wait_ge(s_q1, i + 1)
                    q_transpose1(i, lambda xl: tile(ring_b[:, i % 2, :], xl))
                    kv_product(i)
                if step == 0:
                    gn_mean(2, 0, B // 2, B // 2, bank[7])
                if step == 1:
                    gn_mean(2, 1, B // 2, B // 2, bank[7])
                if step < PAIRS:
                    qkv1(step)

            pe.wait_ge(s_v1, PAIRS)
            conv(1, K1)

            def final(i):
                pe.wait_ge(s_half, PAIRS + i + 1)
                if i >= 1:
                    pe.wait_ge(s_y, i)
                product(bank[2][:, :], wpt[:, 0, :], half0[:, i, :], stop=False)
                product(bank[2][:, :], wpt[:, 1, :], ring_a[:, i % 2, :], start=False).then_inc(s_fin, 1)

            pe.wait_ge(s_ce, 2 + NG)
            for step in range(PAIRS + 3):
                if 0 <= step - 3 < PAIRS:
                    final(step - 3)
                if 0 <= step - 2 < PAIRS:
                    o_transpose(PAIRS + step - 2)
                if 0 <= step - 1 < PAIRS:
                    attend1(PAIRS + step - 1)
                if step < PAIRS:
                    q_transpose1(PAIRS + step, lambda xl: cpos[:, 0, step, xl])
                    kv_product(PAIRS + step)


_INS = ["x", "L0_conv_g_norm", "L0_conv_q_w1", "L0_conv_q_dw", "L0_conv_k_w1", "L0_conv_k_dw", "L0_conv_v_w1",
        "L0_conv_v_dw", "L0_conv_out_w", "L0_conv_g_out", "L1_conv_w_qkv", "L1_conv_w_dw", "L1_conv_w_pw",
        "L1_conv_w_proj", "L1_conv_bn_gamma", "L1_conv_bn_beta", "L1_conv_bn_mean", "L1_conv_bn_var"]


def kernel(**inputs):
    import numpy as _np
    import concourse.bacc as _bacc
    from concourse import mybir as _mybir
    from concourse.bass_utils import run_bass_kernel_spmd as _run

    nc = _bacc.Bacc("TRN2", target_bir_lowering=False, num_devices=1)
    arrays, args = {}, []
    for name in _INS:
        a = _np.ascontiguousarray(inputs[name])
        arrays[f"in_{name}_dram"] = a
        args.append(nc.dram_tensor(f"in_{name}_dram", a.shape, _mybir.dt.from_np(a.dtype), kind="ExternalInput").ap())
    shape = inputs["x"].shape
    args.append(nc.dram_tensor("out_dram", shape, _mybir.dt.float32, kind="ExternalOutput").ap())
    conv_blocks_kernel(nc, *args)
    r = _run(nc, [arrays], core_ids=[0])
    return r.results[0]["out_dram"]
```

```python
from contextlib import ExitStack

import concourse.bass as bass
from concourse import mybir

F32 = mybir.dt.float32
F32R = mybir.dt.float32r
I32 = mybir.dt.int32
ALU = mybir.AluOpType
ACT = mybir.ActivationFunctionType
AX = mybir.AxisListType

P = 128
C = 128
B, HH, WW = 16, 16, 16
NPOS = HH * WW
PAIRS = B // 2
PC = 2 * NPOS
XL, XH = 4, 4
CG = 8
NG = 3 * C // CG
GT = C // CG
HD0 = 16
HD1 = 8
NH1 = C // HD1
K0, K1 = 3, 5
PITCH0 = WW + K0 // 2
PITCH1 = WW + K1 // 2
PAD = 16
TSLOTS = 4
EPS = 1e-5
ATT_EPS = 1e-15
RSQRT_MAGIC = 1597463007.0
NEWTON = 3


def conv_blocks_kernel(nc, x, g_norm, q_w1, q_dw, k_w1, k_dw, v_w1, v_dw, out_w, g_out,
                       w_qkv, w_dw, w_pw, w_proj, bn_gamma, bn_beta, bn_mean, bn_var, out):
    ctx = ExitStack()
    with ctx:
        def sb(name, shape, dt=F32):
            return ctx.enter_context(nc.sbuf_tensor(name, shape, dt))

        def sem(name):
            return ctx.enter_context(nc.semaphore(name))

        xin = sb("xin", [P, B * NPOS])
        half0 = xin[:, :].rearrange("p (i n) -> p i n", i=PAIRS)
        xres = sb("xres", [P, PAIRS, PC])
        cin = sb("cin", [P, NG, B * HH])
        cpos = sb("cpos", [P, 3, PAIRS, XL, C])
        tband = sb("tband", [P, TSLOTS, K1 * C])
        taps1 = sb("taps1", [P, NG * K1 * PITCH1])
        ring_v = sb("ring_v", [P, 2, 2, XL, C + 1])
        ctxm = sb("ctxm", [P, 2, 2, C + NH1])
        zflat = cpos[0:CG].rearrange("p t i x c -> p (t i x c)")
        Z1, W0 = 4096, 8704
        zrow0 = zflat[:, 0:2 * PAD + NG * K0 * PITCH0]
        zrow1 = zflat[:, Z1:Z1 + 2 * PAD + NG * K1 * PITCH1]
        w0t = sb("w0t", [P, 3 * C])
        owt = sb("owt", [P, C])
        w1t = sb("w1t", [P, 3 * C])
        wpt = sb("wpt", [P, 2, C])
        pw = sb("pw", [P, NG, CG])
        ident = sb("ident", [P, P])
        mean4 = sb("mean4", [P, P])
        mask16 = sb("mask16", [P, P])
        mask8 = sb("mask8", [P, P])
        mask_c = sb("mask_c", [P, CG])
        mask_b = sb("mask_b", [P, 2])
        vecs = sb("vecs", [P, 6])
        bn_inv = sb("bn_inv", [P, 1])
        bn_bias = sb("bn_bias", [P, 1])
        gstats = sb("gstats", [P, B, 6])
        gmv = sb("gmv", [P, B, 2])
        gtmp = sb("gtmp", [P, 3, B])
        newt = sb("newt", [P, 3, B])
        gn_s = sb("gn_s", [P, B])
        gn_b = sb("gn_b", [P, B])
        lstats = sb("lstats", [P, XL, 6])
        lmv = sb("lmv", [P, 2, XL, 2])
        lnt = sb("lnt", [P, 3, XL])
        ln_s = sb("ln_s", [P, 2, XL])
        ln_b = sb("ln_b", [P, 2, XL])
        kneg = sb("kneg", [P, B])
        ksum = sb("ksum", [P, B])
        krec = sb("krec", [P, B])
        qmax = sb("qmax", [P, PAIRS * XL])
        qsum = sb("qsum", [P, PAIRS * XL])
        den = sb("den", [P, 2, 2, 2, NH1])
        cflat = cpos[:, :, :, :, :].rearrange("p t i x c -> p (t i x c)")
        wst = [cflat[:, W0 + n * C:W0 + (n + 1) * C] for n in range(9)]
        wproj = cflat[:, W0 + 7 * C:W0 + 9 * C]
        pwst = cflat[:, W0 + 9 * C:W0 + 9 * C + 3 * CG].rearrange("p (t c) -> p t c", t=3)
        pwrep = cflat[:, W0 + 10 * C:W0 + 13 * C].rearrange("p (t x c) -> p t x c", t=3, x=WW)
        dwst0 = cflat[0:CG, W0 + 13 * C:W0 + 13 * C + NG * K0 * K0]
        dwst1 = cflat[0:CG, W0 + 17 * C:W0 + 17 * C + NG * K1 * K1]

        with nc.sbuf_tensor("rings", [P, 5, 2, PC], F32) as rings:
            ring_a, ring_b, ring_c, ring_d, ring_e = (rings[:, n] for n in range(5))
        band_parts = sb("band_parts", [P, TSLOTS, 2, K1 * C], F32R)
        with nc.sbuf_tensor("taps0", [P, NG * K0 * PITCH0], F32) as taps0:
            pass
        cin_parts = sb("cin_parts", [P, TSLOTS, 2, B * HH], F32R)

        bank = [ctx.enter_context(nc.psum_tensor(f"bank{n}", [P, 512], F32)) for n in range(8)]

        s_x = [sem(f"x_quarter{n}_loaded") for n in range(4)]
        s_w0 = sem("block0_weights_loaded")
        s_w = sem("other_weights_loaded")
        s_dw = sem("taps_loaded")
        s_zero = sem("tap_rows_zeroed")
        s_z0 = sem("tap_rows0_ready")
        s_z1 = sem("tap_rows1_ready")
        s_t0 = sem("taps0_shifted")
        s_t1 = sem("taps1_shifted")
        s_pool = sem("pool_chain")
        s_ident = sem("identity_ready")
        s_const = sem("block_masks_ready")
        s_mask = sem("small_masks_ready")
        s_bnw = sem("bn_folded")
        s_wt = sem("weights_transposed")
        s_wte = sem("weights_out_of_psum")
        s_chain = sem("dve_chain")
        s_gnv = sem("gn_operand_ready")
        s_gnp = sem("gn_product_done")
        s_gn = sem("gn_ready")
        s_xp = sem("residual_ready")
        s_xg = sem("a_xg_ready")
        s_xgt = sem("a_xg_transposed")
        s_nrm_t = sem("a_normed_transposed")
        s_xn = sem("a_xn_ready")
        s_lmv = sem("ln_moments_ready")
        s_ln = sem("ln_ready")
        s_nrm = sem("normed_ready")
        s_qkv = sem("qkv_unit_done")
        s_cin = sem("conv_in_unit_ready")
        s_tb = sem("band_ready")
        s_hi = sem("high_parts_ready")
        s_lo = sem("low_parts_ready")
        s_grp = sem("conv_groups_done")
        s_ce = sem("conv_banks_free")
        s_qs = sem("a_q_shifted")
        s_qe = sem("a_q_exp")
        s_qn = sem("a_q_normed")
        s_kq = sem("a_kq_transposed")
        s_kn = sem("a_k_max_ready")
        s_ke = sem("a_k_exp_ready")
        s_qc = sem("a_q_channel_major")
        s_kt = sem("a_k_back_transposed")
        s_kp = sem("a_k_pos_major")
        s_vm = sem("a_v_masked")
        s_cx = sem("a_ctx_done")
        s_cm = sem("a_ctx_masked")
        s_o = sem("a_attn_done")
        s_th = sem("a_tanh_ready")
        s_sl = sem("a_silu_ready")
        s_pr = sem("a_proj_done")
        s_zt = sem("a_z_transposed")
        s_x1 = sem("x1_ready")
        s_xg1 = sem("b_xg_ready")
        s_q1 = sem("b_q_ready")
        s_k1 = sem("b_k_ready")
        s_v1 = sem("b_v_ready")
        s_kv = sem("b_kv_done")
        s_kvm = sem("b_kv_masked")
        s_qt1 = sem("b_q_transposed")
        s_qc1 = sem("b_q_channel_major")
        s_num = sem("b_attn_done")
        s_div = sem("b_attn_divided")
        s_ot = sem("b_attn_transposed")
        s_half = sem("b_attn_channel_major")
        s_fin = sem("b_proj_done")
        s_y = sem("y_ready")
        s_yp = sem("y_natural")
        s_out = [sem(f"out_stored_{n}") for n in ("even", "odd")]

        block = ctx.enter_context(nc.Block())

        def tile(t, xl):
            return t[:, xl * P:(xl + 1) * P]

        def image(t, b):
            return t.rearrange("p (n y b) -> p n y b", b=2, y=HH)[:, :, :, b]

        def image3(t, b):
            return t.rearrange("p (l h y b) -> p l h y b", l=XL, h=XH, b=2)[:, :, :, :, b]

        def natural(t):
            return t.rearrange("p (y h l) -> p l h y", h=XH, l=XL)

        def head_q(h):
            return cpos[:, 0, :, :, h * HD0:(h + 1) * HD0].rearrange("p i x d -> p (i x) d")

        @block.sync
        def _(sp):
            for n in range(4):
                sp.dma_start(xin[:, n * 1024:(n + 1) * 1024].rearrange("p (b n) -> p b n", b=4),
                             x[4 * n:4 * n + 4].rearrange("b c h w -> c b (h w)")).then_inc(s_x[n], 16)
            for zrow, taps, ks, ready, done in ((zrow0, taps0, K0, s_z0, s_t0), (zrow1, taps1, K1, s_z1, s_t1)):
                sp.wait_ge(ready, 1)
                for xi in range(WW):
                    o = PAD + ks // 2 - xi
                    sp.dma_start(taps[CG * xi:CG * (xi + 1), :],
                                 zrow[:, o:o + taps.shape[1]]).then_inc(done, 16)
            for i in range(PAIRS):
                sp.wait_ge(s_yp, i + 1)
                sp.dma_start(out[2 * i:2 * i + 2].rearrange("b c h w -> c b (h w)"),
                             ring_b[:, i % 2, :].rearrange("p (b n) -> p b n", b=2)).then_inc(s_out[i % 2], 16)
            for n in range(2):
                sp.wait_ge(s_out[n], 16 * PAIRS // 2)

        @block.gpsimd
        def _(pool):
            g = nc.gpsimd
            links = [0]

            def link(ins):
                links[0] += 1
                ins.then_inc(s_pool, 1)
                pool.wait_ge(s_pool, links[0])

            g.memset(mean4[:, :], 1.0 / 4)
            link(g.memset(ident[:, :], 0.0))
            g.affine_select(out=ident[:, :], in_=ident[:, :], compare_op=ALU.not_equal, fill=1.0,
                            base=0, pattern=[[-1, P]], channel_multiplier=1).then_inc(s_ident, 1)

            def block_diagonal(m, w):
                mw = m[:, :].rearrange("p (n w) -> p n w", w=w)
                link(g.affine_select(out=mw, in_=mw, compare_op=ALU.is_ge, fill=0.0, base=0,
                                     pattern=[[-w, P // w], [0, w]], channel_multiplier=1))
                return g.affine_select(out=mw, in_=mw, compare_op=ALU.is_ge, fill=0.0, base=w - 1,
                                       pattern=[[w, P // w], [0, w]], channel_multiplier=-1)

            block_diagonal(mean4, 4).then_inc(s_const, 1)
            g.memset(zrow0, 0.0).then_inc(s_zero, 1)
            g.memset(zrow1, 0.0).then_inc(s_zero, 1)
            g.memset(mask16[:, :], float(HD0) ** -0.5)
            link(g.memset(mask8[:, :], 1.0))
            block_diagonal(mask16, HD0)
            block_diagonal(mask8, HD1).then_inc(s_const, 1)

            def layernorm(n):
                w, y, t = lnt[:, 0, :], lnt[:, 1, :], lnt[:, 2, :]
                scale, mean, var = ln_s[:, n % 2, :], lmv[:, n % 2, :, 0], lmv[:, n % 2, :, 1]
                pool.wait_ge(s_lmv, n + 1)
                link(g.tensor_scalar(w, var, EPS, 1.0, ALU.add, ALU.mult))
                link(g.tensor_scalar(y.bitcast(I32), w.bitcast(I32), -0.5, RSQRT_MAGIC, ALU.mult, ALU.add))
                for k in range(NEWTON):
                    link(g.tensor_tensor(out=t, in0=y, in1=y, op=ALU.mult))
                    link(g.tensor_tensor(out=t, in0=t, in1=w, op=ALU.mult))
                    link(g.tensor_scalar(t, t, -0.5, 1.5, ALU.mult, ALU.add))
                    if k == NEWTON - 1 and n >= 2:
                        pool.wait_ge(s_nrm, n - 1)
                    link(g.tensor_tensor(out=y if k < NEWTON - 1 else scale, in0=t, in1=y, op=ALU.mult))
                link(g.tensor_tensor(out=ln_b[:, n % 2, :], in0=mean, in1=scale, op=ALU.mult))
                g.tensor_scalar(ln_b[:, n % 2, :], ln_b[:, n % 2, :], -1.0, 1.0, ALU.mult, ALU.mult).then_inc(s_ln, 1)

            for i in range(PAIRS):
                layernorm(i)

            pool.wait_ge(s_t0, 16 * WW)
            pool.wait_ge(s_mask, 1)
            d0 = taps0[:, :].rearrange("p (g k n) -> p g k n", g=NG, k=K0)
            with pool.Fori(0, NG // TSLOTS) as it:
                for j in range(TSLOTS):
                    pool.wait_ge(s_grp, it * TSLOTS + (j + 1))
                    src = d0[:, bass.ds(it * TSLOTS + j, 1), :, 0:WW].rearrange("p g k n -> p (g k) n")
                    g.tensor_tensor(out=tband[:, j, 0:K0 * C].rearrange("p (k x o) -> p k x o", k=K0, o=CG),
                                    in0=src.unsqueeze(3).broadcast_to([P, K0, WW, CG]),
                                    in1=mask_c[:, :].unsqueeze(1).unsqueeze(1).broadcast_to([P, K0, WW, CG]),
                                    op=ALU.mult).then_inc(s_tb, 1)

            def mask_v(i, ready):
                for b in range(2):
                    last = g.tensor_scalar(ring_v[:, i % 2, b, :, 0:C], cpos[:, 2, i], mask_b[:, b:b + 1], 1.0,
                                           ALU.mult, ALU.mult)
                last.then_inc(ready, 1)

            pool.wait_ge(s_ce, 2 + NG // 2)
            for step in range(PAIRS + 4):
                if step < PAIRS:
                    if step >= 2:
                        pool.wait_ge(s_cx, step - 1)
                    mask_v(step, s_vm)
                if 0 <= step - 4 < PAIRS:
                    layernorm(PAIRS + step - 4)

            pool.wait_ge(s_t1, 16 * WW)
            pool.wait_ge(s_wte, 2)
            d1 = taps1[:, :].rearrange("p (h t k n) -> p h t k n", t=3, k=K1, n=PITCH1)
            pwv = pw[:, :, :].rearrange("p (h t) o -> p h t o", t=3)
            for t in range(3):
                with pool.Fori(0, GT // TSLOTS) as it:
                    for j in range(TSLOTS):
                        pool.wait_ge(s_lo, it * TSLOTS + (t * GT + j + 1))
                        src = d1[:, bass.ds(it * TSLOTS + j, 1), t, :, 0:WW].rearrange("p h k n -> p (h k) n")
                        w = pwv[:, bass.ds(it * TSLOTS + j, 1), t, :]
                        g.tensor_tensor(out=tband[:, j, :].rearrange("p (k x o) -> p k x o", k=K1, o=CG),
                                        in0=src.unsqueeze(3).broadcast_to([P, K1, WW, CG]),
                                        in1=w.unsqueeze(1).broadcast_to([P, K1, WW, CG]),
                                        op=ALU.mult).then_inc(s_tb, 1)

            pool.wait_ge(s_ce, 2 + NG)
            for i in range(PAIRS):
                pool.wait_ge(s_kv, PAIRS + i - 1)
                mask_v(i, s_v1)

        @block.scalar
        def _(act):
            a = nc.scalar
            for n, w in enumerate((q_w1, k_w1, v_w1, out_w)):
                act.dma_start(wst[n], w).then_inc(s_w0, 16)
            act.dma_start(vecs[:, 0:1], g_norm.rearrange("(c a) -> c a", a=1)).then_inc(s_w0, 16)
            for t, w in enumerate((q_dw, k_dw, v_dw)):
                n = GT * K0 * K0
                act.dma_start(dwst0[:, t * n:(t + 1) * n].rearrange("c (g k) -> c g k", g=GT),
                              w.rearrange("(g c) a h w -> c g (a h w)", c=CG)).then_inc(s_dw, 16)
            act.dma_start(dwst1.rearrange("c (g k) -> c g k", g=NG),
                          w_dw.rearrange("(g c) a h w -> c g (a h w)", c=CG)).then_inc(s_dw, 16)
            act.dma_start(cflat[:, W0 + 4 * C:W0 + 7 * C].rearrange("p (t c) -> p t c", t=3),
                          w_qkv.rearrange("(t p) c -> p t c", t=3)).then_inc(s_w, 16)
            act.dma_start(wproj, w_proj).then_inc(s_w, 16)
            act.dma_start(pwst, w_pw.rearrange("(t p) c h w -> p t (c h w)", t=3)).then_inc(s_w, 16)
            for n, vec in enumerate((g_out, bn_gamma, bn_beta, bn_mean, bn_var)):
                act.dma_start(vecs[:, n + 1:n + 2], vec.rearrange("(c a) -> c a", a=1)).then_inc(s_w, 16)

            act.wait_ge(s_wt, 1)
            act.wait_ge(s_w0, 16 * 5)
            a.activation(w0t[:, :], bank[0][:, 0:3 * C], ACT.Copy, scale=vecs[:, 0:1])
            a.mul(owt[:, :], bank[0][:, 3 * C:4 * C], 0.5)
            a.copy(w1t[:, :], bank[1][:, 0:3 * C]).then_inc(s_wte, 1)

            def normed(n, src, dst):
                act.wait_ge(s_ln, n + 1)
                for xl in range(XL):
                    last = a.activation(tile(dst, xl), tile(src, xl), ACT.Identity,
                                        scale=ln_s[:, n % 2, xl:xl + 1], bias=ln_b[:, n % 2, xl:xl + 1])
                last.then_inc(s_nrm, 1)

            def xg(i):
                if i >= 2:
                    act.wait_ge(s_xgt, i - 1)
                for b in range(2):
                    n = 2 * i + b
                    last = a.activation(image3(ring_a[:, i % 2, :], b), natural(xin[:, n * NPOS:(n + 1) * NPOS]),
                                        ACT.Identity, scale=gn_s[:, n:n + 1], bias=gn_b[:, n:n + 1])
                last.then_inc(s_xg, 1)

            def front_normed(i):
                if i >= 2:
                    act.wait_ge(s_nrm_t, i - 1)
                normed(i, bank[i % 2][:, :], ring_b[:, i % 2, :])

            def xn(i):
                act.wait_ge(s_nrm_t, i + 1)
                if i >= 2:
                    act.wait_ge(s_qkv, 3 * (i - 1))
                a.copy(ring_c[:, i % 2, :], bank[2 + i % 2][:, :]).then_inc(s_xn, 1)

            for step in range(PAIRS + 3):
                if step < PAIRS:
                    act.wait_ge(s_gn, 1 + step // (PAIRS // 2))
                    xg(step)
                if 0 <= step - 3 < PAIRS:
                    xn(step - 3)
                if 0 <= step - 2 < PAIRS:
                    front_normed(step - 2)

            act.wait_ge(s_wt, 2)
            a.copy(pw[:, :, :].rearrange("p g c -> p (g c)"), bank[2][:, 0:3 * C])
            a.copy(wpt[:, :, :].rearrange("p t c -> p (t c)"), bank[3][:, 0:2 * C]).then_inc(s_wte, 1)

            for h in range(C // HD0):
                for b in range(2):
                    last = a.copy(image3(xres[:, h, :], b), natural(xin[:, (2 * h + b) * NPOS:(2 * h + b + 1) * NPOS]))
                last.then_inc(s_xp, 1)
                act.wait_ge(s_qs, h + 1)
                a.activation(head_q(h), head_q(h), ACT.Exp).then_inc(s_qe, 1)

            def k_exp(i):
                act.wait_ge(s_kn, i + 1)
                if i >= 2:
                    act.wait_ge(s_kt, i - 1)
                for b in range(2):
                    n = 2 * i + b
                    last = a.activation(image(ring_a[:, i % 2, :], b), image(bank[0][:, :], b), ACT.Exp,
                                        bias=kneg[:, n:n + 1], accum_out=ksum[:, n:n + 1])
                last.then_inc(s_ke, 1)

            def q_out(i):
                if i >= 2:
                    act.wait_ge(s_o, i - 1)
                a.copy(ring_b[:, i % 2, :], bank[1][:, :]).then_inc(s_qc, 1)

            def k_out(i):
                act.wait_ge(s_kt, i + 1)
                if i >= 2:
                    act.wait_ge(s_cx, i - 1)
                a.copy(ring_c[:, i % 2, :], bank[2][:, :]).then_inc(s_kp, 1)

            def tanh(i):
                act.wait_ge(s_o, i + 1)
                if i >= 2:
                    act.wait_ge(s_pr, i - 1)
                a.activation(ring_d[:, i % 2, :], bank[4][:, :], ACT.Tanh, scale=0.5).then_inc(s_th, 1)

            def z_normed(i):
                if i >= 2:
                    act.wait_ge(s_zt, i - 1)
                normed(PAIRS + i, bank[5 + i % 2][:, :], ring_e[:, i % 2, :])

            for step in range(PAIRS + 5):
                if 0 <= step - 3 < PAIRS:
                    tanh(step - 3)
                if 0 <= step - 1 < PAIRS:
                    q_out(step - 1)
                    k_out(step - 1)
                if 0 <= step - 5 < PAIRS:
                    z_normed(step - 5)
                if step < PAIRS:
                    k_exp(step)

            def xg1(i):
                act.wait_ge(s_gn, 3 + i // (PAIRS // 2))
                act.wait_ge(s_kt, PAIRS) if i < 2 else act.wait_ge(s_qkv, 3 * PAIRS + 3 * (i - 1))
                for b in range(2):
                    n = 2 * i + b
                    last = a.activation(image(ring_a[:, i % 2, :], b), image(xres[:, i, :], b),
                                        ACT.Identity, scale=gn_s[:, n:n + 1], bias=gn_b[:, n:n + 1])
                last.then_inc(s_xg1, 1)

            def front1(i):
                act.wait_ge(s_cin, 3 * PAIRS + 3 * i + 1)
                act.wait_ge(s_o, PAIRS) if i < 2 else act.wait_ge(s_qt1, i - 1)
                a.activation(ring_b[:, i % 2, :], bank[0][:, :], ACT.Relu).then_inc(s_q1, 1)
                act.wait_ge(s_cin, 3 * PAIRS + 3 * i + 2)
                act.wait_ge(s_cx, PAIRS) if i < 2 else act.wait_ge(s_kv, i - 1)
                a.activation(ring_c[:, i % 2, :], bank[1][:, :], ACT.Relu).then_inc(s_k1, 1)
                act.wait_ge(s_cin, 3 * PAIRS + 3 * i + 3)
                for b in range(2):
                    last = a.activation(ring_v[:, i % 2, b, :, 0:C],
                                        bank[2][:, :].rearrange("p (x c) -> p x c", x=XL),
                                        ACT.Copy, scale=mask_b[:, b:b + 1])
                last.then_inc(s_v1, 1)

            def q_out1(n):
                act.wait_ge(s_qt1, n + 1)
                act.wait_ge(s_pr, PAIRS) if n < 2 else act.wait_ge(s_num, n - 1)
                a.activation(ring_d[:, n % 2, :].rearrange("p (b n y) -> p b n y", b=2, y=HH),
                             bank[3][:, :].rearrange("p (n y b) -> p b n y", b=2, y=HH),
                             ACT.Copy if n < PAIRS else ACT.Relu).then_inc(s_qc1, 1)

            def half_out(i):
                act.wait_ge(s_ot, i + 1)
                a.copy(half0[:, i, :], bank[7][:, :]).then_inc(s_half, 1)

            xg1(0)
            for step in range(PAIRS + 5):
                if 0 <= step - 4 < PAIRS:
                    half_out(step - 4)
                if 0 <= step - 1 < PAIRS:
                    q_out1(step - 1)
                if step + 1 < PAIRS:
                    xg1(step + 1)
                if step < PAIRS:
                    front1(step)

            act.wait_ge(s_num, PAIRS)
            act.wait_ge(s_ot, PAIRS)
            for g in range(NG):
                if g >= TSLOTS:
                    act.wait_ge(s_grp, NG + g + 1)
                a.copy(cin_parts[:, g % TSLOTS, 0, :], cin[:, g, :])
                act.wait_ge(s_tb, NG + g + 1)
                a.copy(band_parts[:, g % TSLOTS, 0, :], tband[:, g % TSLOTS, :]).then_inc(s_hi, 1)

            def k_relu(i):
                act.wait_ge(s_kv, PAIRS + i - 1)
                a.activation(ring_c[:, i % 2, :], cpos[:, 1, i].rearrange("p x c -> p (x c)"),
                             ACT.Relu).then_inc(s_k1, 1)

            def half1_out(i):
                act.wait_ge(s_ot, PAIRS + i + 1)
                if i >= 2:
                    act.wait_ge(s_fin, i - 1)
                a.copy(ring_a[:, i % 2, :], bank[7][:, :]).then_inc(s_half, 1)

            def y_out(i):
                act.wait_ge(s_y, i + 1)
                if i >= 2:
                    act.wait_ge(s_out[i % 2], 16 * (i // 2))
                for b in range(2):
                    last = a.copy(natural(ring_b[:, i % 2, b * NPOS:(b + 1) * NPOS]), image3(xres[:, i, :], b))
                last.then_inc(s_yp, 1)

            act.wait_ge(s_ce, 2 + NG)
            for step in range(PAIRS + 4):
                if 0 <= step - 4 < PAIRS:
                    y_out(step - 4)
                if 0 <= step - 2 < PAIRS:
                    half1_out(step - 2)
                if step < PAIRS:
                    k_relu(step)
                    q_out1(PAIRS + step)

        @block.vector
        def _(dve):
            v = nc.vector
            links = [0]

            def link(ins, meanwhile=None):
                links[0] += 1
                n = links[0]
                ins.then_inc(s_chain, 1)
                if meanwhile:
                    meanwhile.pop(0)()
                dve.wait_ge(s_chain, n)

            def rsqrt(dst, var, n, work=None):
                w, y, t = newt[:, 0, 0:n], newt[:, 1, 0:n], newt[:, 2, 0:n]
                link(v.tensor_scalar(w, var, EPS, None, ALU.add), work)
                link(v.tensor_scalar(y.bitcast(I32), w.bitcast(I32), -0.5, RSQRT_MAGIC, ALU.mult, ALU.add), work)
                for k in range(NEWTON):
                    link(v.tensor_tensor(t, y, y, ALU.mult), work)
                    link(v.scalar_tensor_tensor(out=t, in0=t, scalar=-0.5, in1=w, op0=ALU.mult, op1=ALU.mult), work)
                    link(v.scalar_tensor_tensor(out=y if k < NEWTON - 1 else dst, in0=t, scalar=1.5, in1=y,
                                                op0=ALU.add, op1=ALU.mult), work)

            def tap_rows():
                dve.wait_ge(s_dw, 16 * 4)
                for n, (zrow, st, ks, pitch, ready) in enumerate(((zrow0, dwst0, K0, PITCH0, s_z0),
                                                                  (zrow1, dwst1, K1, PITCH1, s_z1))):
                    dve.wait_ge(s_zero, n + 1)
                    rows = zrow[:, PAD:PAD + NG * ks * pitch].rearrange("c (r n) -> c r n", n=pitch)
                    v.tensor_copy(rows[:, :, 0:ks],
                                  st.rearrange("c (r k) -> c r k", k=ks)[:, :, ::-1]).then_inc(ready, 1)

            def small_masks():
                v.tensor_reduce(mask_c[:, :], ident[:, :].rearrange("p (j o) -> p o j", o=CG), op=ALU.add, axis=AX.X)
                link(v.tensor_reduce(mask_b[:, :], ident[:, :].rearrange("p (h y b) -> p b h y", h=XH, b=2),
                                     op=ALU.add, axis=AX.XY))
                for s in range(2):
                    for xl in range(XL):
                        last = v.tensor_copy(ring_v[:, s, :, xl, C], mask_b[:, :])
                last.then_inc(s_mask, 1)

            def fold_batchnorm():
                dve.wait_ge(s_w, 16 * 8)
                for t in range(3):
                    v.tensor_copy(pwrep[:, t], pwst[:, t, :].unsqueeze(1).broadcast_to([P, WW, CG]))
                rsqrt(bn_inv[:, :], vecs[:, 5:6], 1)
                link(v.tensor_tensor(bn_bias[:, :], bn_inv[:, :], vecs[:, 2:3], ALU.mult))
                v.tensor_scalar(wproj, wproj, bn_bias[:, :], None, ALU.mult).then_inc(s_bnw, 1)
                link(v.tensor_tensor(bn_inv[:, :], bn_bias[:, :], vecs[:, 4:5], ALU.mult))
                v.tensor_tensor(bn_bias[:, :], vecs[:, 3:4], bn_inv[:, :], ALU.subtract)

            def gn_aggregate(c, b0, n):
                for b in range(b0, b0 + n):
                    last = v.bn_aggr(gmv[:, b, :], gstats[:, b, :])
                last.then_inc(s_gnv, 1)

            def gn_variance(c, b0, n, ps):
                m, d = gtmp[:, 0, 0:n], gtmp[:, 1, 0:n]
                dve.wait_ge(s_gnp, 2 * c + 1)
                dve.wait_ge(s_gnv, 2 * c + 1)
                link(v.tensor_copy(m, ps[:, 0:n]))
                link(v.tensor_tensor(d, gmv[:, b0:b0 + n, 0], m, ALU.subtract))
                link(v.tensor_tensor(d, d, d, ALU.mult))
                v.tensor_tensor(gmv[:, b0:b0 + n, 1], gmv[:, b0:b0 + n, 1], d, ALU.add).then_inc(s_gnv, 1)

            def gn_scale(c, b0, n, ps):
                dve.wait_ge(s_gnp, 2 * c + 2)
                link(v.tensor_copy(gtmp[:, 2, 0:n], ps[:, B:B + n]))
                rsqrt(gn_s[:, b0:b0 + n], gtmp[:, 2, 0:n], n)
                v.scalar_tensor_tensor(out=gn_b[:, b0:b0 + n], in0=gtmp[:, 0, 0:n], scalar=-1.0,
                                       in1=gn_s[:, b0:b0 + n], op0=ALU.mult, op1=ALU.mult).then_inc(s_gn, 1)

            def moments(n, src, work):
                if n >= 1:
                    dve.wait_ge(s_lmv, n)
                for xl in range(XL):
                    last = v.bn_stats(lstats[:, xl, :], tile(src, xl))
                link(last, work)
                if n >= 2:
                    dve.wait_ge(s_ln, n - 1)
                for xl in range(XL):
                    last = v.bn_aggr(lmv[:, n % 2, xl, :], lstats[:, xl, :])
                last.then_inc(s_lmv, 1)

            def conv_in(t, i, ps):
                v.transpose(cin[:, t * GT:(t + 1) * GT, 32 * i:32 * i + 32],
                            ps[:, :].rearrange("p (x g c) -> p g x c", x=XL, c=CG)).then_inc(s_cin, 1)

            for c in range(2):
                b0 = c * B // 2
                for b in range(b0, b0 + B // 2):
                    if b % 4 == 0:
                        dve.wait_ge(s_x[b // 4], 16)
                    last = v.bn_stats(gstats[:, b, :], xin[:, b * NPOS:(b + 1) * NPOS])
                link(last)
                gn_aggregate(c, b0, B // 2)
                if c == 0:
                    dve.wait_ge(s_ident, 1)
                    small_masks()
                gn_variance(c, b0, B // 2, bank[7])
                gn_scale(c, b0, B // 2, bank[7])
            tap_rows()
            for step in range(PAIRS + 4):
                work = []
                if 0 <= step - 4 < PAIRS:
                    def unit(t, i=step - 4):
                        u = 3 * i + t
                        dve.wait_ge(s_qkv, u + 1)
                        conv_in(t, i, bank[4 + u % 4])
                    work = [lambda t=t: unit(t) for t in range(3)]
                if step == 2:
                    fold_batchnorm()
                if step < PAIRS:
                    dve.wait_ge(s_xgt, step + 1)
                    moments(step, bank[step % 2][:, :], work)
                for left in work:
                    left()

            def conv_out(n):
                dve.wait_ge(s_grp, TSLOTS + 2 * (n + 1))
                for j in range(2):
                    t, g = divmod((2 * n + j) % NG, GT)
                    last = v.transpose(cpos[:, t, :, :, g * CG:(g + 1) * CG],
                                       bank[n % 2][:, j * B * HH:(j + 1) * B * HH])
                last.then_inc(s_ce, 1)

            def over_head(t):
                return t[:, :].unsqueeze(2).broadcast_to([P, PAIRS * XL, HD0])

            def q_shift(h):
                dve.wait_ge(s_ce, 2 + h + 1)
                if h:
                    dve.wait_ge(s_qs, h)
                link(v.tensor_reduce(qmax[:, :], head_q(h), op=ALU.max, axis=AX.X))
                v.tensor_tensor(head_q(h), head_q(h), over_head(qmax), ALU.subtract).then_inc(s_qs, 1)

            def q_scale(h):
                dve.wait_ge(s_qe, h + 1)
                if h:
                    dve.wait_ge(s_qn, h)
                link(v.tensor_reduce(qsum[:, :], head_q(h), op=ALU.add, axis=AX.X))
                link(v.reciprocal(qsum[:, :], qsum[:, :]))
                v.tensor_tensor(head_q(h), head_q(h), over_head(qsum), ALU.mult).then_inc(s_qn, 1)

            dve.wait_ge(s_t0, 16 * WW)
            dve.wait_ge(s_t1, 16 * WW)
            heads = C // HD0
            for n in range(NG // 2):
                conv_out(n)
                if 1 <= n <= heads:
                    q_shift(n - 1)
                if 3 <= n <= heads + 2:
                    q_scale(n - 3)

            def k_max(i):
                dve.wait_ge(s_kq, i + 1)
                v.tensor_reduce(kneg[:, 2 * i:2 * i + 2],
                                bank[0][:, :].rearrange("p (n y b) -> p b n y", b=2, y=HH),
                                op=ALU.max, axis=AX.XY, negate=True).then_inc(s_kn, 1)

            def ctx_mask(i):
                dve.wait_ge(s_ke, i + 1)
                link(v.reciprocal(krec[:, 2 * i:2 * i + 2], ksum[:, 2 * i:2 * i + 2]))
                dve.wait_ge(s_cx, i + 1)
                if i >= 2:
                    dve.wait_ge(s_o, i - 1)
                for b in range(2):
                    last = v.scalar_tensor_tensor(
                        out=ctxm[:, i % 2, b, 0:C], in0=bank[3][:, b * C:(b + 1) * C],
                        scalar=krec[:, 2 * i + b:2 * i + b + 1], in1=mask16[:, :], op0=ALU.mult, op1=ALU.mult)
                last.then_inc(s_cm, 1)

            def silu(i):
                dve.wait_ge(s_th, i + 1)
                v.scalar_tensor_tensor(out=ring_d[:, i % 2, :], in0=ring_d[:, i % 2, :], scalar=1.0,
                                       in1=bank[4][:, :], op0=ALU.add, op1=ALU.mult).then_inc(s_sl, 1)

            def x1(i):
                dve.wait_ge(s_zt, i + 1)
                dve.wait_ge(s_xp, i + 1)
                v.scalar_tensor_tensor(out=xres[:, i, :], in0=bank[7][:, :], scalar=vecs[:, 1:2],
                                       in1=xres[:, i, :], op0=ALU.mult, op1=ALU.add).then_inc(s_x1, 1)

            def x1_stats(i):
                dve.wait_ge(s_x1, i + 1)
                for b in range(2):
                    last = v.bn_stats(gstats[:, 2 * i + b, :], image(xres[:, i, :], b))
                if i % (PAIRS // 2) == PAIRS // 2 - 1:
                    link(last)
                    gn_aggregate(2 + 2 * i // B, 2 * i + 2 - B // 2, B // 2)

            for step in range(PAIRS + 8):
                work = []
                if 0 <= step - 7 < PAIRS:
                    work.append(lambda: x1(step - 7))
                if 0 <= step - 4 < PAIRS:
                    dve.wait_ge(s_pr, step - 4 + 1)
                    moments(PAIRS + step - 4, bank[5 + step % 2][:, :], work)
                for left in work:
                    left()
                if 0 <= step - 2 < PAIRS:
                    ctx_mask(step - 2)
                if 0 <= step - 7 < PAIRS:
                    x1_stats(step - 7)
                if 0 <= step - 3 < PAIRS:
                    silu(step - 3)
                if step < PAIRS:
                    k_max(step)
                if step == PAIRS // 2 + 7:
                    gn_variance(2, 0, B // 2, bank[3][:, 2 * C:4 * C])
                    gn_scale(2, 0, B // 2, bank[3][:, 2 * C:4 * C])

            def kv_mask(n):
                dve.wait_ge(s_kv, n + 1)
                dve.wait_ge(s_o, PAIRS) if n < 2 else dve.wait_ge(s_num, n - 1)
                for b in range(2):
                    o = b * (C + 1)
                    v.tensor_tensor(ctxm[:, n % 2, b, 0:C], bank[4][:, o:o + C], mask8[:, :], ALU.mult)
                    last = v.tensor_scalar(ctxm[:, n % 2, b, C:C + NH1],
                                           mask8[:, :].rearrange("p (h d) -> p h d", d=HD1)[:, :, 0],
                                           bank[4][:, o + C:o + C + 1], None, ALU.mult)
                last.then_inc(s_kvm, 1)

            def attn_div(n):
                dve.wait_ge(s_num, n + 1)
                dve.wait_ge(s_zt, PAIRS) if n < 2 else dve.wait_ge(s_ot, n - 1)
                s = n % 2
                tiles = [bank[5 + b][:, 0:2 * (C + NH1)].rearrange("p (j c) -> p j c", j=2) for b in range(2)]
                for b in range(2):
                    last = v.tensor_scalar(den[:, s, b, :, :], tiles[b][:, :, C:C + NH1], ATT_EPS, None, ALU.add)
                link(last)
                dv = den[:, s, :, :, :].rearrange("p b j h -> p (b j h)")
                link(v.reciprocal(dv, dv))
                for b in range(2):
                    last = v.tensor_tensor(
                        ring_e[:, s, 2 * b * C:2 * (b + 1) * C].rearrange("p (j h d) -> p j h d", j=2, d=HD1),
                        tiles[b][:, :, 0:C].rearrange("p j (h d) -> p j h d", d=HD1),
                        den[:, s, b, :, :].unsqueeze(3).broadcast_to([P, 2, NH1, HD1]), ALU.mult)
                last.then_inc(s_div, 1)

            for step in range(PAIRS + 4):
                if step == 0:
                    gn_variance(3, B // 2, B // 2, bank[7])
                if step == 1:
                    gn_scale(3, B // 2, B // 2, bank[7])
                if 0 <= step - 3 < PAIRS:
                    attn_div(step - 3)
                if 0 <= step - 2 < PAIRS:
                    kv_mask(step - 2)
                if step < PAIRS:
                    for t in range(3):
                        dve.wait_ge(s_qkv, 3 * PAIRS + 3 * step + t + 1)
                        conv_in(t, step, bank[t])

            def low_parts(g):
                if g >= TSLOTS:
                    dve.wait_ge(s_grp, NG + g + 1)
                dve.wait_ge(s_hi, g + 1)
                for part, whole in ((cin_parts, cin[:, g, :]), (band_parts, tband[:, g % TSLOTS, :])):
                    last = v.tensor_tensor(part[:, g % TSLOTS, 1, :], whole,
                                           part[:, g % TSLOTS, 0, :].bitcast(F32), ALU.subtract)
                last.then_inc(s_lo, 1)

            dve.sem_inc(s_lo, TSLOTS)
            for g in range(3):
                low_parts(g)
            for n in range(NG // 2, NG):
                for g in (2 * (n - NG // 2) + 3, 2 * (n - NG // 2) + 4):
                    if g < NG:
                        low_parts(g)
                conv_out(n)

            def y(i):
                dve.wait_ge(s_fin, i + 1)
                for b in range(2):
                    r = image(xres[:, i, :], b)
                    last = v.scalar_tensor_tensor(
                        out=r, in0=bank[2][:, b * NPOS:(b + 1) * NPOS].rearrange("p (n y) -> p n y", y=HH),
                        scalar=bn_bias[:, :], in1=r, op0=ALU.add, op1=ALU.add)
                last.then_inc(s_y, 1)

            for step in range(PAIRS + 3):
                if 0 <= step - 3 < PAIRS:
                    y(step - 3)
                if 0 <= step - 1 < PAIRS:
                    attn_div(PAIRS + step - 1)
                if step < PAIRS:
                    kv_mask(PAIRS + step)

        @block.tensor
        def _(pe):
            t_ = nc.tensor

            def transposes(dst, src):
                for xl in range(XL):
                    last = t_.transpose(tile(dst, xl), src(xl), ident[:, :])
                return last

            def product(dst, stationary, moving, start=True, stop=True):
                return t_.matmul(dst, stationary, moving, start=start, stop=stop, skip_group_check=True)

            pe.wait_ge(s_ident, 1)
            pe.wait_ge(s_w0, 16 * 5)
            for n in range(4):
                t_.transpose(tile(bank[0], n), wst[n], ident[:, :])
            pe.wait_ge(s_w, 16 * 8)
            for n in range(3):
                last = t_.transpose(tile(bank[1], n), wst[4 + n], ident[:, :])
            last.then_inc(s_wt, 1)

            def gn_mean(c, k, b0, n, ps):
                pe.wait_ge(s_gnv, 2 * c + k + 1)
                product(ps[:, B * k:B * k + n], mean4[:, :], gmv[:, b0:b0 + n, k]).then_inc(s_gnp, 1)

            pe.wait_ge(s_const, 1)
            for c in range(2):
                for k in range(2):
                    if (c, k) == (1, 0):
                        pe.wait_ge(s_gn, 1)
                    gn_mean(c, k, c * B // 2, B // 2, bank[7])
            pe.wait_ge(s_wte, 1)
            for step in range(PAIRS + 4):
                if 0 <= step - 4 < PAIRS:
                    i = step - 4
                    pe.wait_ge(s_xn, i + 1)
                    for t in range(3):
                        u = 3 * i + t
                        if u >= 4:
                            pe.wait_ge(s_cin, u - 3)
                        if u == 3:
                            pe.wait_ge(s_gn, 2)
                        for xl in range(XL):
                            last = product(tile(bank[4 + u % 4], xl), tile(ring_c[:, i % 2, :], xl),
                                           w0t[:, t * C:(t + 1) * C])
                        last.then_inc(s_qkv, 1)
                if 0 <= step - 3 < PAIRS:
                    i = step - 3
                    pe.wait_ge(s_nrm, i + 1)
                    if i >= 2:
                        pe.wait_ge(s_xn, i - 1)
                    transposes(bank[2 + i % 2], lambda xl: tile(ring_b[:, i % 2, :], xl)).then_inc(s_nrm_t, 1)
                if step < PAIRS:
                    i = step
                    pe.wait_ge(s_xg, i + 1)
                    if i >= 2:
                        pe.wait_ge(s_nrm, i - 1)
                    transposes(bank[i % 2], lambda xl: tile(ring_a[:, i % 2, :], xl)).then_inc(s_xgt, 1)

            pe.wait_ge(s_xn, PAIRS)
            pe.wait_ge(s_bnw, 1)
            for n in range(3):
                product(tile(bank[2], n), pwrep[:, n].rearrange("p x c -> p (x c)"), ident[:, :])
            for n in range(2):
                last = t_.transpose(tile(bank[3], n), wst[7 + n], ident[:, :])
            last.then_inc(s_wt, 1)

            def conv(which, ks):
                order = [ks // 2] + [k for k in range(ks) if k != ks // 2]
                with pe.Fori(0, NG // TSLOTS) as it:
                    for j in range(TSLOTS):
                        dst = bank[j // 2][:, (j % 2) * B * HH:(j % 2 + 1) * B * HH].rearrange("p (i n) -> p i n", i=PAIRS)
                        src = cin[:, bass.ds(it * TSLOTS + j, 1), :].rearrange("p g (i n) -> p (g i) n", i=PAIRS)
                        if j % 2 == 0:
                            pe.wait_ge(s_ce, it * 2 + (which * (NG // 2) + j // 2 + 1))
                        pe.wait_ge(s_tb, it * TSLOTS + (which * NG + j + 1))
                        for k in order:
                            dy = k - ks // 2
                            lo, hi = max(0, -dy), min(HH, HH - dy)
                            last = product(dst[:, :, 2 * lo:2 * hi], tband[:, j, k * C:(k + 1) * C], src[:, :, 2 * (lo + dy):2 * (hi + dy)],
                                           start=k == ks // 2, stop=k == order[-1])
                        last.then_inc(s_grp, 1)

            pe.sem_inc(s_grp, TSLOTS)
            pe.sem_inc(s_ce, 2)
            pe.wait_ge(s_nrm, PAIRS)
            pe.wait_ge(s_cin, 3 * PAIRS)
            conv(0, K0)

            def conv_in_parts():
                order = [K1 // 2] + [k for k in range(K1) if k != K1 // 2]
                with pe.Fori(0, NG // TSLOTS) as it:
                    for j in range(TSLOTS):
                        dst = bank[j // 2][:, (j % 2) * B * HH:(j % 2 + 1) * B * HH].rearrange("p (i n) -> p i n", i=PAIRS)
                        if j % 2 == 0:
                            pe.wait_ge(s_ce, it * 2 + (NG // 2 + j // 2 + 1))
                        for q_band, q_in in ((0, 0), (0, 1), (1, 0)):
                            if (q_band, q_in) == (0, 0):
                                pe.wait_ge(s_hi, it * TSLOTS + (j + 1))
                            elif q_in:
                                pe.wait_ge(s_lo, it * TSLOTS + (TSLOTS + j + 1))
                            src = cin_parts[:, j, q_in, :].rearrange("p (i n) -> p i n", i=PAIRS)
                            for k in order:
                                dy = k - K1 // 2
                                lo, hi = max(0, -dy), min(HH, HH - dy)
                                last = product(dst[:, :, 2 * lo:2 * hi],
                                               band_parts[:, j, q_band, k * C:(k + 1) * C],
                                               src[:, :, 2 * (lo + dy):2 * (hi + dy)],
                                               start=(q_band, q_in, k) == (0, 0, K1 // 2),
                                               stop=q_band == 1 and k == order[-1])
                        last.then_inc(s_grp, 1)

            def kq_transpose(i):
                if i == 0:
                    pe.wait_ge(s_ce, 2 + NG // 2)
                    pe.wait_ge(s_qn, C // HD0)
                else:
                    pe.wait_ge(s_ke, i)
                    pe.wait_ge(s_qc, i)
                transposes(bank[0], lambda xl: cpos[:, 1, i, xl])
                transposes(bank[1], lambda xl: cpos[:, 0, i, xl]).then_inc(s_kq, 1)

            def k_back(i):
                pe.wait_ge(s_ke, i + 1)
                if i >= 1:
                    pe.wait_ge(s_kp, i)
                transposes(bank[2], lambda xl: tile(ring_a[:, i % 2, :], xl)).then_inc(s_kt, 1)

            def context(i):
                pe.wait_ge(s_kp, i + 1)
                pe.wait_ge(s_vm, i + 1)
                if i >= 1:
                    pe.wait_ge(s_cm, i)
                for xl in range(XL):
                    last = product(bank[3][:, 0:2 * C], tile(ring_c[:, i % 2, :], xl), ring_v[:, i % 2, :, xl, 0:C],
                                   start=xl == 0, stop=xl == XL - 1)
                last.then_inc(s_cx, 1)

            def attend(i):
                pe.wait_ge(s_cm, i + 1)
                pe.wait_ge(s_qc, i + 1)
                if i >= 1:
                    pe.wait_ge(s_sl, i)
                for b in range(2):
                    last = product(image(bank[4][:, :], b), ctxm[:, i % 2, b, 0:C], image(ring_b[:, i % 2, :], b))
                last.then_inc(s_o, 1)

            def project(i):
                pe.wait_ge(s_sl, i + 1)
                if i >= 2:
                    pe.wait_ge(s_nrm, PAIRS + i - 1)
                for xl in range(XL):
                    last = product(tile(bank[5 + i % 2], xl), tile(ring_d[:, i % 2, :], xl), owt[:, :])
                last.then_inc(s_pr, 1)

            def z_transpose(i):
                pe.wait_ge(s_nrm, PAIRS + i + 1)
                if i >= 1:
                    pe.wait_ge(s_x1, i)
                transposes(bank[7], lambda xl: tile(ring_e[:, i % 2, :], xl)).then_inc(s_zt, 1)

            pe.wait_ge(s_wte, 2)
            gn_bank = bank[3][:, 2 * C:4 * C]
            for step in range(PAIRS + 7):
                if step == PAIRS // 2 + 7:
                    gn_mean(2, 0, 0, B // 2, gn_bank)
                if 0 <= step - 7 < PAIRS:
                    z_transpose(step - 7)
                if 0 <= step - 4 < PAIRS:
                    project(step - 4)
                if 0 <= step - 3 < PAIRS:
                    attend(step - 3)
                if 0 <= step - 2 < PAIRS:
                    context(step - 2)
                if 0 <= step - 1 < PAIRS:
                    k_back(step - 1)
                if step < PAIRS:
                    kq_transpose(step)
                if step == PAIRS // 2 + 7:
                    gn_mean(2, 1, 0, B // 2, gn_bank)

            def qkv1(i):
                pe.wait_ge(s_xg1, i + 1)
                w = w1t[:, :].rearrange("p (h t e) -> p t h e", t=3, e=HD1)
                for t, (free, free0) in enumerate(((s_q1, s_qc), (s_k1, s_kp), (s_v1, s_kp))):
                    if i == 0:
                        pe.wait_ge(s_ke, PAIRS)
                        pe.wait_ge(free0, PAIRS)
                    else:
                        pe.wait_ge(free, i)
                    for xl in range(XL):
                        last = product(tile(bank[t], xl), tile(ring_a[:, i % 2, :], xl), w[:, t])
                    last.then_inc(s_qkv, 1)

            def q_transpose1(n, src):
                if n == 0:
                    pe.wait_ge(s_cm, PAIRS)
                else:
                    pe.wait_ge(s_qc1, n)
                transposes(bank[3], src).then_inc(s_qt1, 1)

            def kv_product(n):
                pe.wait_ge(s_k1, n + 1)
                pe.wait_ge(s_v1, n + 1)
                if n == 0:
                    pe.wait_ge(s_sl, PAIRS)
                else:
                    pe.wait_ge(s_kvm, n)
                for xl in range(XL):
                    last = product(bank[4][:, 0:2 * (C + 1)], tile(ring_c[:, n % 2, :], xl), ring_v[:, n % 2, :, xl, :],
                                   start=xl == 0, stop=xl == XL - 1)
                last.then_inc(s_kv, 1)

            def attend1(n):
                pe.wait_ge(s_kvm, n + 1)
                pe.wait_ge(s_qc1, n + 1)
                if n == 0:
                    pe.wait_ge(s_nrm, 2 * PAIRS)
                    pe.wait_ge(s_gn, 3)
                else:
                    pe.wait_ge(s_div, n)
                for b in range(2):
                    for j in range(2):
                        last = product(bank[5 + b][:, j * (C + NH1):(j + 1) * (C + NH1)],
                                       tile(ring_d[:, n % 2, :], 2 * b + j), ctxm[:, n % 2, b, :])
                last.then_inc(s_num, 1)

            def o_transpose(n):
                pe.wait_ge(s_div, n + 1)
                if n == 0:
                    pe.wait_ge(s_gn, 4)
                else:
                    pe.wait_ge(s_half, n)
                transposes(bank[7], lambda xl: tile(ring_e[:, n % 2, :], xl)).then_inc(s_ot, 1)

            for step in range(PAIRS + 5):
                if step == 0:
                    gn_mean(3, 0, B // 2, B // 2, bank[7])
                if 0 <= step - 4 < PAIRS:
                    o_transpose(step - 4)
                if 0 <= step - 3 < PAIRS:
                    attend1(step - 3)
                if 0 <= step - 2 < PAIRS:
                    kv_product(step - 2)
                if 0 <= step - 1 < PAIRS:
                    pe.wait_ge(s_q1, step)
                    q_transpose1(step - 1, lambda xl: tile(ring_b[:, (step - 1) % 2, :], xl))
                if step < PAIRS:
                    qkv1(step)
                if step == 0:
                    gn_mean(3, 1, B // 2, B // 2, bank[7])

            pe.wait_ge(s_v1, PAIRS)
            conv_in_parts()

            def final(i):
                pe.wait_ge(s_half, PAIRS + i + 1)
                if i >= 1:
                    pe.wait_ge(s_y, i)
                product(bank[2][:, :], wpt[:, 0, :], half0[:, i, :], stop=False)
                product(bank[2][:, :], wpt[:, 1, :], ring_a[:, i % 2, :], start=False).then_inc(s_fin, 1)

            pe.wait_ge(s_ce, 2 + NG)
            for step in range(PAIRS + 3):
                if 0 <= step - 3 < PAIRS:
                    final(step - 3)
                if 0 <= step - 2 < PAIRS:
                    o_transpose(PAIRS + step - 2)
                if 0 <= step - 1 < PAIRS:
                    attend1(PAIRS + step - 1)
                if step < PAIRS:
                    q_transpose1(PAIRS + step, lambda xl: cpos[:, 0, step, xl])
                    kv_product(PAIRS + step)


_INS = ["x", "L0_conv_g_norm", "L0_conv_q_w1", "L0_conv_q_dw", "L0_conv_k_w1", "L0_conv_k_dw", "L0_conv_v_w1",
        "L0_conv_v_dw", "L0_conv_out_w", "L0_conv_g_out", "L1_conv_w_qkv", "L1_conv_w_dw", "L1_conv_w_pw",
        "L1_conv_w_proj", "L1_conv_bn_gamma", "L1_conv_bn_beta", "L1_conv_bn_mean", "L1_conv_bn_var"]


def kernel(**inputs):
    import numpy as _np
    import concourse.bacc as _bacc
    from concourse import mybir as _mybir
    from concourse.bass_utils import run_bass_kernel_spmd as _run

    nc = _bacc.Bacc("TRN2", target_bir_lowering=False, num_devices=1)
    arrays, args = {}, []
    for name in _INS:
        a = _np.ascontiguousarray(inputs[name])
        arrays[f"in_{name}_dram"] = a
        args.append(nc.dram_tensor(f"in_{name}_dram", a.shape, _mybir.dt.from_np(a.dtype), kind="ExternalInput").ap())
    shape = inputs["x"].shape
    args.append(nc.dram_tensor("out_dram", shape, _mybir.dt.float32, kind="ExternalOutput").ap())
    conv_blocks_kernel(nc, *args)
    r = _run(nc, [arrays], core_ids=[0])
    return r.results[0]["out_dram"]
```

```python
from contextlib import ExitStack

import concourse.bass as bass
from concourse import mybir

F32 = mybir.dt.float32
F32R = mybir.dt.float32r
I32 = mybir.dt.int32
ALU = mybir.AluOpType
ACT = mybir.ActivationFunctionType
AX = mybir.AxisListType

P = 128
C = 128
B, HH, WW = 16, 16, 16
NPOS = HH * WW
PAIRS = B // 2
PC = 2 * NPOS
XL, XH = 4, 4
CG = 8
NG = 3 * C // CG
GT = C // CG
HD0 = 16
HD1 = 8
NH1 = C // HD1
K0, K1 = 3, 5
PITCH0 = WW + K0 // 2
PITCH1 = WW + K1 // 2
PAD = 16
FRONT1 = 11
X_BANKS = 0, 1, 3
CONV_BANKS = 2, 0
HIGH_EARLY = 3
LOW_EARLY = 2
CONV1_STEPS = 10, 11, 11, 11
GN1 = ((0, 2, 8), (2, 5, 11), (5, 8, 14))
TSLOTS = 4
EPS = 1e-5
ATT_EPS = 1e-15
RSQRT_MAGIC = 1595932665.0
N0, N1 = -0.703952253, 0.703952253 * 2.38924456
H0, H1, H2 = 0.375, -1.25, 1.875


def conv_blocks_kernel(nc, x, g_norm, q_w1, q_dw, k_w1, k_dw, v_w1, v_dw, out_w, g_out,
                       w_qkv, w_dw, w_pw, w_proj, bn_gamma, bn_beta, bn_mean, bn_var, out):
    ctx = ExitStack()
    with ctx:
        def sb(name, shape, dt=F32):
            return ctx.enter_context(nc.sbuf_tensor(name, shape, dt))

        def sem(name):
            return ctx.enter_context(nc.semaphore(name))

        xin = sb("xin", [P, B * NPOS])
        half0 = xin[:, :].rearrange("p (i n) -> p i n", i=PAIRS)
        xres = sb("xres", [P, PAIRS, PC])
        cpos = sb("cpos", [P, 3, PAIRS, XL, C])
        tband = sb("tband", [P, TSLOTS, K1 * C])
        taps1 = sb("taps1", [P, NG * K1 * PITCH1])
        ring_v = sb("ring_v", [P, 2, 2, XL, C + 1])
        ctxm = sb("ctxm", [P, 2, 2, C + NH1])
        zflat = cpos[0:CG].rearrange("p t i x c -> p (t i x c)")
        Z1, W0 = 4096, 8704
        zrow0 = zflat[:, 0:2 * PAD + NG * K0 * PITCH0]
        zrow1 = zflat[:, Z1:Z1 + 2 * PAD + NG * K1 * PITCH1]
        w0t = sb("w0t", [P, 3 * C])
        owt = sb("owt", [P, C])
        w1t = sb("w1t", [P, 3 * C])
        wpt = sb("wpt", [P, 2, C])
        pw = sb("pw", [P, NG, CG])
        ident = sb("ident", [P, P])
        mean4 = sb("mean4", [P, P])
        mask16 = sb("mask16", [P, P])
        mask8 = sb("mask8", [P, P])
        mask_c = sb("mask_c", [P, CG])
        mask_b = sb("mask_b", [P, 2])
        vecs = sb("vecs", [P, 6])
        bn_inv = sb("bn_inv", [P, 1])
        bn_bias = sb("bn_bias", [P, 1])
        gstats = sb("gstats", [P, B, 6])
        gmv = sb("gmv", [P, B, 2])
        gtmp = sb("gtmp", [P, 3, B])
        newt = sb("newt", [P, 3, B])
        gn_s = sb("gn_s", [P, B])
        gn_b = sb("gn_b", [P, B])
        lstats = sb("lstats", [P, XL, 6])
        lmv = sb("lmv", [P, 2, XL, 2])
        lnt = sb("lnt", [P, 4, XL])
        ln_s = sb("ln_s", [P, 2, XL])
        ln_b = sb("ln_b", [P, 2, XL])
        kneg = sb("kneg", [P, B])
        ksum = sb("ksum", [P, B])
        krec = sb("krec", [P, B])
        qmax = sb("qmax", [P, PAIRS * XL])
        qsum = sb("qsum", [P, PAIRS * XL])
        den = sb("den", [P, 2, 2, 2, NH1])
        cflat = cpos[:, :, :, :, :].rearrange("p t i x c -> p (t i x c)")
        wst = [cflat[:, W0 + n * C:W0 + (n + 1) * C] for n in range(9)]
        wproj = cflat[:, W0 + 7 * C:W0 + 9 * C]
        pwst = cflat[:, W0 + 9 * C:W0 + 9 * C + 3 * CG].rearrange("p (t c) -> p t c", t=3)
        pwrep = cflat[:, W0 + 10 * C:W0 + 13 * C].rearrange("p (t x c) -> p t x c", t=3, x=WW)
        dwst0 = cflat[0:CG, W0 + 13 * C:W0 + 13 * C + NG * K0 * K0]
        dwst1 = cflat[0:CG, W0 + 17 * C:W0 + 17 * C + NG * K1 * K1]

        with nc.sbuf_tensor("rings", [P, 5, 2, PC], F32) as rings:
            ring_a, ring_b, ring_c, ring_d, ring_e = (rings[:, n] for n in range(5))
        band_parts = sb("band_parts", [P, TSLOTS, 2, K1 * C], F32R)
        with nc.sbuf_tensor("cin", [P, NG, B * HH], F32) as cin:
            pass
        proj_parts = sb("proj_parts", [P, 2, 2, 2, PC], F32R)
        w_parts = sb("w_parts", [P, 2, 2, C], F32R)
        sb("rest_of_cin", [P, NG * B * HH - 8 * PC - 4 * C])
        with nc.sbuf_tensor("taps0", [P, NG * K0 * PITCH0], F32) as taps0:
            pass
        cin_parts = sb("cin_parts", [P, TSLOTS, 2, B * HH], F32R)

        bank = [ctx.enter_context(nc.psum_tensor(f"bank{n}", [P, 512], F32)) for n in range(8)]

        gn_sums = bank[0], bank[4], bank[7]

        s_x = [sem(f"x_quarter{n}_loaded") for n in range(4)]
        s_w0 = sem("block0_weights_loaded")
        s_w = sem("other_weights_loaded")
        s_dw = sem("taps_loaded")
        s_zero = sem("tap_rows_zeroed")
        s_z0 = sem("tap_rows0_ready")
        s_z1 = sem("tap_rows1_ready")
        s_t0 = sem("taps0_shifted")
        s_t1 = sem("taps1_shifted")
        s_pool = sem("pool_chain")
        s_ident = sem("identity_ready")
        s_const = sem("block_masks_ready")
        s_mask = sem("small_masks_ready")
        s_bnw = sem("bn_folded")
        s_wt = sem("weights_transposed")
        s_wte = sem("weights_out_of_psum")
        s_chain = sem("dve_chain")
        s_gnv = sem("gn_operand_ready")
        s_gnp = sem("gn_product_done")
        s_gn = sem("gn_ready")
        s_xp = sem("residual_ready")
        s_xg = sem("a_xg_ready")
        s_xgt = sem("a_xg_transposed")
        s_nrm_t = sem("a_normed_transposed")
        s_xn = sem("a_xn_ready")
        s_lmv = sem("ln_moments_ready")
        s_ln = sem("ln_ready")
        s_nrm = sem("normed_ready")
        s_qkv = sem("qkv_unit_done")
        s_cin = sem("conv_in_unit_ready")
        s_tb = sem("band_ready")
        s_hi = sem("high_parts_ready")
        s_lo = sem("low_parts_ready")
        s_grp = sem("conv_groups_done")
        s_ce = sem("conv_banks_free")
        s_qs = sem("a_q_shifted")
        s_qe = sem("a_q_exp")
        s_qn = sem("a_q_normed")
        s_kq = sem("a_kq_transposed")
        s_kn = sem("a_k_max_ready")
        s_ke = sem("a_k_exp_ready")
        s_qc = sem("a_q_channel_major")
        s_kt = sem("a_k_back_transposed")
        s_kp = sem("a_k_pos_major")
        s_vm = sem("a_v_masked")
        s_cx = sem("a_ctx_done")
        s_cm = sem("a_ctx_masked")
        s_o = sem("a_attn_done")
        s_th = sem("a_tanh_ready")
        s_sl = sem("a_silu_ready")
        s_pr = sem("a_proj_done")
        s_zt = sem("a_z_transposed")
        s_x1 = sem("x1_ready")
        s_xg1 = sem("b_xg_ready")
        s_q1 = sem("b_q_ready")
        s_k1 = sem("b_k_ready")
        s_v1 = sem("b_v_ready")
        s_vfirst = sem("b_v_of_second_halfs_first_pair_ready")
        s_kv = sem("b_kv_done")
        s_kvm = sem("b_kv_masked")
        s_qt1 = sem("b_q_transposed")
        s_qc1 = sem("b_q_channel_major")
        s_num = sem("b_attn_done")
        s_div = sem("b_attn_divided")
        s_ot = sem("b_attn_transposed")
        s_half = sem("b_attn_channel_major")
        s_h0 = sem("c_first_half_high_ready")
        s_p0 = sem("c_first_half_parts_ready")
        s_p1 = sem("c_second_half_parts_ready")
        s_whi = sem("c_weights_high_ready")
        s_fin = sem("b_proj_done")
        s_y = sem("y_ready")
        s_yp = sem("y_natural")
        s_out = [sem(f"out_stored_{n}") for n in ("even", "odd")]

        block = ctx.enter_context(nc.Block())

        def tile(t, xl):
            return t[:, xl * P:(xl + 1) * P]

        def image(t, b):
            return t.rearrange("p (n y b) -> p n y b", b=2, y=HH)[:, :, :, b]

        def image3(t, b):
            return t.rearrange("p (l h y b) -> p l h y b", l=XL, h=XH, b=2)[:, :, :, :, b]

        def natural(t):
            return t.rearrange("p (y h l) -> p l h y", h=XH, l=XL)

        def head_q(h):
            return cpos[:, 0, :, :, h * HD0:(h + 1) * HD0].rearrange("p i x d -> p (i x) d")

        @block.sync
        def _(sp):
            for n in range(4):
                sp.dma_start(xin[:, n * 1024:(n + 1) * 1024].rearrange("p (b n) -> p b n", b=4),
                             x[4 * n:4 * n + 4].rearrange("b c h w -> c b (h w)")).then_inc(s_x[n], 16)
            for zrow, taps, ks, ready, done in ((zrow0, taps0, K0, s_z0, s_t0), (zrow1, taps1, K1, s_z1, s_t1)):
                sp.wait_ge(ready, 1)
                for xi in range(WW):
                    o = PAD + ks // 2 - xi
                    sp.dma_start(taps[CG * xi:CG * (xi + 1), :],
                                 zrow[:, o:o + taps.shape[1]]).then_inc(done, 16)
            for i in range(PAIRS):
                sp.wait_ge(s_yp, i + 1)
                sp.dma_start(out[2 * i:2 * i + 2].rearrange("b c h w -> c b (h w)"),
                             ring_b[:, i % 2, :].rearrange("p (b n) -> p b n", b=2)).then_inc(s_out[i % 2], 16)
            for n in range(2):
                sp.wait_ge(s_out[n], 16 * PAIRS // 2)

        @block.gpsimd
        def _(pool):
            g = nc.gpsimd
            links = [0]

            def link(ins):
                links[0] += 1
                ins.then_inc(s_pool, 1)
                pool.wait_ge(s_pool, links[0])

            g.memset(mean4[:, :], 1.0 / 4)
            link(g.memset(ident[:, :], 0.0))
            g.affine_select(out=ident[:, :], in_=ident[:, :], compare_op=ALU.not_equal, fill=1.0,
                            base=0, pattern=[[-1, P]], channel_multiplier=1).then_inc(s_ident, 1)

            def block_diagonal(m, w):
                mw = m[:, :].rearrange("p (n w) -> p n w", w=w)
                link(g.affine_select(out=mw, in_=mw, compare_op=ALU.is_ge, fill=0.0, base=0,
                                     pattern=[[-w, P // w], [0, w]], channel_multiplier=1))
                return g.affine_select(out=mw, in_=mw, compare_op=ALU.is_ge, fill=0.0, base=w - 1,
                                       pattern=[[w, P // w], [0, w]], channel_multiplier=-1)

            block_diagonal(mean4, 4).then_inc(s_const, 1)
            g.memset(zrow0, 0.0).then_inc(s_zero, 1)
            g.memset(zrow1, 0.0).then_inc(s_zero, 1)
            g.memset(mask16[:, :], float(HD0) ** -0.5)
            link(g.memset(mask8[:, :], 1.0))
            block_diagonal(mask16, HD0)
            block_diagonal(mask8, HD1).then_inc(s_const, 1)

            def layernorm(n):
                w, y, t, less = (lnt[:, k, :] for k in range(4))
                scale, mean, var = ln_s[:, n % 2, :], lmv[:, n % 2, :, 0], lmv[:, n % 2, :, 1]
                pool.wait_ge(s_lmv, n + 1)
                if n >= 1:
                    pool.wait_ge(s_ln, n)
                g.tensor_scalar(less, mean, -1.0, 1.0, ALU.mult, ALU.mult)
                link(g.tensor_scalar(w, var, EPS, 1.0, ALU.add, ALU.mult))
                link(g.tensor_scalar(y.bitcast(I32), w.bitcast(I32), -0.5, RSQRT_MAGIC, ALU.mult, ALU.add))
                link(g.tensor_tensor(out=t, in0=y, in1=y, op=ALU.mult))
                link(g.tensor_tensor(out=t, in0=t, in1=w, op=ALU.mult))
                link(g.tensor_scalar(t, t, N0, N1, ALU.mult, ALU.add))
                link(g.tensor_tensor(out=y, in0=y, in1=t, op=ALU.mult))
                link(g.tensor_tensor(out=t, in0=y, in1=y, op=ALU.mult))
                link(g.tensor_tensor(out=t, in0=t, in1=w, op=ALU.mult))
                link(g.tensor_scalar(w, t, H0, H1, ALU.mult, ALU.add))
                link(g.tensor_tensor(out=t, in0=t, in1=w, op=ALU.mult))
                link(g.tensor_scalar(t, t, H2, 1.0, ALU.add, ALU.mult))
                if n >= 2:
                    pool.wait_ge(s_nrm, n - 1)
                link(g.tensor_tensor(out=scale, in0=t, in1=y, op=ALU.mult))
                g.tensor_tensor(out=ln_b[:, n % 2, :], in0=less, in1=scale, op=ALU.mult).then_inc(s_ln, 1)

            for i in range(PAIRS):
                layernorm(i)

            pool.wait_ge(s_t0, 16 * WW)
            pool.wait_ge(s_mask, 1)
            d0 = taps0[:, :].rearrange("p (g k n) -> p g k n", g=NG, k=K0)
            with pool.Fori(0, NG // TSLOTS) as it:
                for j in range(TSLOTS):
                    pool.wait_ge(s_grp, it * TSLOTS + (j + 1))
                    src = d0[:, bass.ds(it * TSLOTS + j, 1), :, 0:WW].rearrange("p g k n -> p (g k) n")
                    g.tensor_tensor(out=tband[:, j, 0:K0 * C].rearrange("p (k x o) -> p k x o", k=K0, o=CG),
                                    in0=src.unsqueeze(3).broadcast_to([P, K0, WW, CG]),
                                    in1=mask_c[:, :].unsqueeze(1).unsqueeze(1).broadcast_to([P, K0, WW, CG]),
                                    op=ALU.mult).then_inc(s_tb, 1)

            def mask_v(i, ready):
                for b in range(2):
                    last = g.tensor_scalar(ring_v[:, i % 2, b, :, 0:C], cpos[:, 2, i], mask_b[:, b:b + 1], 1.0,
                                           ALU.mult, ALU.mult)
                last.then_inc(ready, 1)

            pool.wait_ge(s_ce, 2 + NG // 2)
            for step in range(PAIRS + 4):
                if step < PAIRS:
                    if step >= 2:
                        pool.wait_ge(s_cx, step - 1)
                    mask_v(step, s_vm)
                if 0 <= step - 4 < PAIRS:
                    layernorm(PAIRS + step - 4)

            pool.wait_ge(s_t1, 16 * WW)
            pool.wait_ge(s_wte, 2)
            d1 = taps1[:, :].rearrange("p (h t k n) -> p h t k n", t=3, k=K1, n=PITCH1)
            pwv = pw[:, :, :].rearrange("p (h t) o -> p h t o", t=3)
            for t in range(3):
                with pool.Fori(0, GT // TSLOTS) as it:
                    for j in range(TSLOTS):
                        pool.wait_ge(s_lo, it * TSLOTS + (t * GT + j + 1))
                        src = d1[:, bass.ds(it * TSLOTS + j, 1), t, :, 0:WW].rearrange("p h k n -> p (h k) n")
                        w = pwv[:, bass.ds(it * TSLOTS + j, 1), t, :]
                        g.tensor_tensor(out=tband[:, j, :].rearrange("p (k x o) -> p k x o", k=K1, o=CG),
                                        in0=src.unsqueeze(3).broadcast_to([P, K1, WW, CG]),
                                        in1=w.unsqueeze(1).broadcast_to([P, K1, WW, CG]),
                                        op=ALU.mult).then_inc(s_tb, 1)

            pool.wait_ge(s_ce, 2 + NG)
            for i in range(1, PAIRS):
                pool.wait_ge(s_kv, PAIRS + i - 1)
                mask_v(i, s_v1)

        @block.scalar
        def _(act):
            a = nc.scalar
            for n, w in enumerate((q_w1, k_w1, v_w1, out_w)):
                act.dma_start(wst[n], w).then_inc(s_w0, 16)
            act.dma_start(vecs[:, 0:1], g_norm.rearrange("(c a) -> c a", a=1)).then_inc(s_w0, 16)
            for t, w in enumerate((q_dw, k_dw, v_dw)):
                n = GT * K0 * K0
                act.dma_start(dwst0[:, t * n:(t + 1) * n].rearrange("c (g k) -> c g k", g=GT),
                              w.rearrange("(g c) a h w -> c g (a h w)", c=CG)).then_inc(s_dw, 16)
            act.dma_start(dwst1.rearrange("c (g k) -> c g k", g=NG),
                          w_dw.rearrange("(g c) a h w -> c g (a h w)", c=CG)).then_inc(s_dw, 16)
            act.dma_start(cflat[:, W0 + 4 * C:W0 + 7 * C].rearrange("p (t c) -> p t c", t=3),
                          w_qkv.rearrange("(t p) c -> p t c", t=3)).then_inc(s_w, 16)
            act.dma_start(wproj, w_proj).then_inc(s_w, 16)
            act.dma_start(pwst, w_pw.rearrange("(t p) c h w -> p t (c h w)", t=3)).then_inc(s_w, 16)
            for n, vec in enumerate((g_out, bn_gamma, bn_beta, bn_mean, bn_var)):
                act.dma_start(vecs[:, n + 1:n + 2], vec.rearrange("(c a) -> c a", a=1)).then_inc(s_w, 16)

            act.wait_ge(s_ident, 1)
            a.activation(kneg[:, 0:1], ident[:, 0:1], ACT.Exp)

            act.wait_ge(s_wt, 1)
            act.wait_ge(s_w0, 16 * 5)
            a.activation(w0t[:, :], bank[0][:, 0:3 * C], ACT.Copy, scale=vecs[:, 0:1])
            a.mul(owt[:, :], bank[0][:, 3 * C:4 * C], 0.5).then_inc(s_wte, 1)

            def normed(n, src, dst):
                act.wait_ge(s_ln, n + 1)
                for xl in range(XL):
                    last = a.activation(tile(dst, xl), tile(src, xl), ACT.Identity,
                                        scale=ln_s[:, n % 2, xl:xl + 1], bias=ln_b[:, n % 2, xl:xl + 1])
                last.then_inc(s_nrm, 1)

            def xg(i):
                if i >= 2:
                    act.wait_ge(s_xgt, i - 1)
                for b in range(2):
                    n = 2 * i + b
                    last = a.activation(image3(ring_a[:, i % 2, :], b), natural(xin[:, n * NPOS:(n + 1) * NPOS]),
                                        ACT.Identity, scale=gn_s[:, n:n + 1], bias=gn_b[:, n:n + 1])
                last.then_inc(s_xg, 1)

            def front_normed(i):
                if i >= 2:
                    act.wait_ge(s_nrm_t, i - 1)
                normed(i, bank[X_BANKS[i % 3]][:, :], ring_b[:, i % 2, :])

            def xn(i):
                act.wait_ge(s_nrm_t, i + 1)
                if i >= 2:
                    act.wait_ge(s_qkv, 3 * (i - 1))
                a.copy(ring_c[:, i % 2, :], bank[2][:, :]).then_inc(s_xn, 1)

            act.wait_ge(s_gn, 1)
            xg(0)
            for step in range(PAIRS + 2):
                if step + 1 < PAIRS:
                    if step + 1 == PAIRS // 2:
                        act.wait_ge(s_gn, 2)
                    xg(step + 1)
                if 0 <= step - 2 < PAIRS:
                    xn(step - 2)
                if 0 <= step - 1 < PAIRS:
                    front_normed(step - 1)

            act.wait_ge(s_wt, 2)
            a.copy(w1t[:, :], bank[4][:, 0:3 * C])
            a.copy(pw[:, :, :].rearrange("p g c -> p (g c)"), bank[0][:, 0:3 * C])
            a.copy(wpt[:, :, :].rearrange("p t c -> p (t c)"), bank[1][:, 0:2 * C]).then_inc(s_wte, 1)

            for h in range(C // HD0):
                for b in range(2):
                    last = a.copy(image3(xres[:, h, :], b), natural(xin[:, (2 * h + b) * NPOS:(2 * h + b + 1) * NPOS]))
                last.then_inc(s_xp, 1)
                act.wait_ge(s_qs, h + 1)
                a.activation(head_q(h), head_q(h), ACT.Exp).then_inc(s_qe, 1)

            def k_exp(i):
                act.wait_ge(s_kn, i + 1)
                if i >= 2:
                    act.wait_ge(s_kt, i - 1)
                for b in range(2):
                    n = 2 * i + b
                    last = a.activation(image(ring_a[:, i % 2, :], b), image(bank[0][:, :], b), ACT.Exp,
                                        bias=kneg[:, n:n + 1], accum_out=ksum[:, n:n + 1])
                last.then_inc(s_ke, 1)

            def q_out(i):
                if i >= 2:
                    act.wait_ge(s_o, i - 1)
                a.copy(ring_b[:, i % 2, :], bank[1][:, :]).then_inc(s_qc, 1)

            def k_out(i):
                act.wait_ge(s_kt, i + 1)
                if i >= 2:
                    act.wait_ge(s_cx, i - 1)
                a.copy(ring_c[:, i % 2, :], bank[2][:, :]).then_inc(s_kp, 1)

            def tanh(i):
                act.wait_ge(s_o, i + 1)
                if i >= 2:
                    act.wait_ge(s_pr, i - 1)
                a.activation(ring_d[:, i % 2, :], bank[4][:, :], ACT.Tanh, scale=0.5).then_inc(s_th, 1)

            def z_normed(i):
                if i >= 2:
                    act.wait_ge(s_zt, i - 1)
                normed(PAIRS + i, bank[5 + i % 2][:, :], ring_e[:, i % 2, :])

            def xg1(i):
                act.wait_ge(s_gn, 3 + [i < i1 for i0, i1, _ in GN1].index(True))
                act.wait_ge(s_kt, PAIRS) if i < 2 else act.wait_ge(s_qkv, 3 * PAIRS + 3 * (i - 1))
                for b in range(2):
                    n = 2 * i + b
                    last = a.activation(image(ring_a[:, i % 2, :], b), image(xres[:, i, :], b),
                                        ACT.Identity, scale=gn_s[:, n:n + 1], bias=gn_b[:, n:n + 1])
                last.then_inc(s_xg1, 1)

            def front1(i):
                act.wait_ge(s_cin, 3 * PAIRS + 3 * i + 1)
                act.wait_ge(s_o, PAIRS) if i < 2 else act.wait_ge(s_qt1, i - 1)
                a.activation(ring_b[:, i % 2, :], bank[0][:, :], ACT.Relu).then_inc(s_q1, 1)
                act.wait_ge(s_cin, 3 * PAIRS + 3 * i + 2)
                act.wait_ge(s_cx, PAIRS) if i < 2 else act.wait_ge(s_kv, i - 1)
                a.activation(ring_c[:, i % 2, :], bank[1][:, :], ACT.Relu).then_inc(s_k1, 1)
                act.wait_ge(s_cin, 3 * PAIRS + 3 * i + 3)
                for b in range(2):
                    last = a.activation(ring_v[:, i % 2, b, :, 0:C],
                                        bank[2][:, :].rearrange("p (x c) -> p x c", x=XL),
                                        ACT.Copy, scale=mask_b[:, b:b + 1])
                last.then_inc(s_v1, 1)

            def q_out1(n):
                act.wait_ge(s_qt1, n + 1)
                act.wait_ge(s_pr, PAIRS) if n < 2 else act.wait_ge(s_num, n - 1)
                a.activation(ring_d[:, n % 2, :].rearrange("p (b n y) -> p b n y", b=2, y=HH),
                             bank[3][:, :].rearrange("p (n y b) -> p b n y", b=2, y=HH),
                             ACT.Copy if n < PAIRS else ACT.Relu).then_inc(s_qc1, 1)

            def half_out(i):
                act.wait_ge(s_ot, i + 1)
                a.copy(half0[:, i, :], bank[7][:, :]).then_inc(s_half, 1)

            def high_parts(g):
                if g < TSLOTS:
                    act.wait_ge((s_qt1, s_kv, s_num, s_ot)[g], PAIRS)
                else:
                    act.wait_ge(s_grp, NG + g + 1)
                act.wait_ge(s_cin, 6 * PAIRS)
                a.copy(cin_parts[:, g % TSLOTS, 0, :], cin[:, g, :])
                act.wait_ge(s_tb, NG + g + 1)
                a.copy(band_parts[:, g % TSLOTS, 0, :], tband[:, g % TSLOTS, :]).then_inc(s_hi, 1)

            for step in range(FRONT1 + PAIRS + 4):
                if 0 <= step - 3 < PAIRS:
                    tanh(step - 3)
                if 0 <= step - 1 < PAIRS:
                    q_out(step - 1)
                if 0 <= step - 5 < PAIRS:
                    z_normed(step - 5)
                if 0 <= step - 1 < PAIRS:
                    k_out(step - 1)
                if step < PAIRS:
                    k_exp(step)
                n = step - FRONT1
                if 0 <= n - 1 < PAIRS:
                    q_out1(n - 1)
                if 0 <= n - 4 < PAIRS:
                    half_out(n - 4)
                if 0 <= n < PAIRS:
                    front1(n)
                if 0 <= n + 1 < PAIRS:
                    xg1(n + 1)
                if 0 <= n - PAIRS < HIGH_EARLY:
                    high_parts(n - PAIRS)

            def k_relu(i):
                if i == 0:
                    act.wait_ge(s_ce, 2 + NG // 2 + 2 * GT // 2)
                k = cpos[:, 1, i].rearrange("p x c -> p (x c)")
                a.activation(k, k, ACT.Relu).then_inc(s_k1, 1)

            for g in range(HIGH_EARLY, NG):
                high_parts(g)
                if 0 <= g - (2 * GT + 5) < PAIRS:
                    k_relu(g - (2 * GT + 5))

            def half1_out(i):
                act.wait_ge(s_ot, PAIRS + i + 1)
                a.copy(proj_parts[:, i % 2, 1, 0, :], bank[7][:, :]).then_inc(s_half, 1)

            def half0_high(i):
                if i >= 2:
                    act.wait_ge(s_fin, i - 1)
                a.copy(proj_parts[:, i % 2, 0, 0, :], half0[:, i, :]).then_inc(s_h0, 1)

            def y_out(i):
                act.wait_ge(s_y, i + 1)
                if i >= 2:
                    act.wait_ge(s_out[i % 2], 16 * (i // 2))
                for b in range(2):
                    last = a.copy(natural(ring_b[:, i % 2, b * NPOS:(b + 1) * NPOS]), image3(xres[:, i, :], b))
                last.then_inc(s_yp, 1)

            act.wait_ge(s_lo, TSLOTS + NG)
            a.copy(w_parts[:, :, 0, :], wpt[:, :, :]).then_inc(s_whi, 1)
            half0_high(0)
            act.wait_ge(s_grp, TSLOTS + 2 * NG)
            for step in range(PAIRS + 4):
                if 0 <= step - 4 < PAIRS:
                    y_out(step - 4)
                if 0 <= step - 2 < PAIRS:
                    half1_out(step - 2)
                if 1 <= step - 1 < PAIRS:
                    half0_high(step - 1)
                if step < PAIRS:
                    q_out1(PAIRS + step)

        @block.vector
        def _(dve):
            v = nc.vector
            links = [0]

            def link(ins, meanwhile=None):
                links[0] += 1
                n = links[0]
                ins.then_inc(s_chain, 1)
                if meanwhile:
                    meanwhile.pop(0)()
                dve.wait_ge(s_chain, n)

            def rsqrt(dst, var, n, work=None):
                w, y, t = newt[:, 0, 0:n], newt[:, 1, 0:n], newt[:, 2, 0:n]
                link(v.tensor_scalar(w, var, EPS, None, ALU.add), work)
                link(v.tensor_scalar(y.bitcast(I32), w.bitcast(I32), -0.5, RSQRT_MAGIC, ALU.mult, ALU.add), work)
                link(v.tensor_tensor(t, y, y, ALU.mult), work)
                link(v.tensor_tensor(t, t, w, ALU.mult), work)
                link(v.scalar_tensor_tensor(out=y, in0=t, scalar=N1 / N0, in1=y, op0=ALU.add, op1=ALU.mult), work)
                link(v.tensor_tensor(t, y, y, ALU.mult), work)
                link(v.scalar_tensor_tensor(out=t, in0=t, scalar=N0 * N0, in1=w, op0=ALU.mult, op1=ALU.mult), work)
                link(v.tensor_scalar(w, t, N0 * H0, N0 * H1, ALU.mult, ALU.add), work)
                link(v.tensor_tensor(t, t, w, ALU.mult), work)
                link(v.scalar_tensor_tensor(out=dst, in0=t, scalar=N0 * H2, in1=y, op0=ALU.add, op1=ALU.mult), work)

            def tap_rows():
                dve.wait_ge(s_dw, 16 * 4)
                for n, (zrow, st, ks, pitch, ready) in enumerate(((zrow0, dwst0, K0, PITCH0, s_z0),
                                                                  (zrow1, dwst1, K1, PITCH1, s_z1))):
                    dve.wait_ge(s_zero, n + 1)
                    rows = zrow[:, PAD:PAD + NG * ks * pitch].rearrange("c (r n) -> c r n", n=pitch)
                    v.tensor_copy(rows[:, :, 0:ks],
                                  st.rearrange("c (r k) -> c r k", k=ks)[:, :, ::-1]).then_inc(ready, 1)

            def small_masks():
                v.tensor_reduce(mask_c[:, :], ident[:, :].rearrange("p (j o) -> p o j", o=CG), op=ALU.add, axis=AX.X)
                link(v.tensor_reduce(mask_b[:, :], ident[:, :].rearrange("p (h y b) -> p b h y", h=XH, b=2),
                                     op=ALU.add, axis=AX.XY))
                for s in range(2):
                    for xl in range(XL):
                        last = v.tensor_copy(ring_v[:, s, :, xl, C], mask_b[:, :])
                last.then_inc(s_mask, 1)

            def fold_batchnorm():
                dve.wait_ge(s_w, 16 * 8)
                for t in range(3):
                    v.tensor_copy(pwrep[:, t], pwst[:, t, :].unsqueeze(1).broadcast_to([P, WW, CG]))
                rsqrt(bn_inv[:, :], vecs[:, 5:6], 1)
                link(v.tensor_tensor(bn_bias[:, :], bn_inv[:, :], vecs[:, 2:3], ALU.mult))
                v.tensor_scalar(wproj, wproj, bn_bias[:, :], None, ALU.mult).then_inc(s_bnw, 1)
                link(v.tensor_tensor(bn_inv[:, :], bn_bias[:, :], vecs[:, 4:5], ALU.mult))
                v.tensor_tensor(bn_bias[:, :], vecs[:, 3:4], bn_inv[:, :], ALU.subtract)

            def gn_aggregate(c, b0, n):
                for b in range(b0, b0 + n):
                    last = v.bn_aggr(gmv[:, b, :], gstats[:, b, :])
                last.then_inc(s_gnv, 1)

            def gn_variance(c, b0, n, ps):
                m, d = gtmp[:, 0, 0:n], gtmp[:, 1, 0:n]
                dve.wait_ge(s_gnp, 2 * c + 1)
                dve.wait_ge(s_gnv, 2 * c + 1)
                link(v.tensor_copy(m, ps[:, 0:n]))
                link(v.tensor_tensor(d, gmv[:, b0:b0 + n, 0], m, ALU.subtract))
                link(v.tensor_tensor(d, d, d, ALU.mult))
                v.tensor_tensor(gmv[:, b0:b0 + n, 1], gmv[:, b0:b0 + n, 1], d, ALU.add).then_inc(s_gnv, 1)

            def gn_scale(c, b0, n, ps, work=None):
                dve.wait_ge(s_gnp, 2 * c + 2)
                link(v.tensor_copy(gtmp[:, 2, 0:n], ps[:, B:B + n]))
                rsqrt(gn_s[:, b0:b0 + n], gtmp[:, 2, 0:n], n, work)
                v.scalar_tensor_tensor(out=gn_b[:, b0:b0 + n], in0=gtmp[:, 0, 0:n], scalar=-1.0,
                                       in1=gn_s[:, b0:b0 + n], op0=ALU.mult, op1=ALU.mult).then_inc(s_gn, 1)

            def tile_stats(n, src, xl):
                if xl == 0:
                    if n >= 1:
                        dve.wait_ge(s_lmv, n)
                    dve.wait_ge(s_xgt, n + 1) if n < PAIRS else dve.wait_ge(s_pr, n - PAIRS + 1)
                return v.bn_stats(lstats[:, xl, :], tile(src, xl))

            def moments(n, src, work, begun=0):
                for xl in range(begun, XL):
                    last = tile_stats(n, src, xl)
                link(last, work)
                if n >= 2:
                    dve.wait_ge(s_ln, n - 1)
                for xl in range(XL):
                    last = v.bn_aggr(lmv[:, n % 2, xl, :], lstats[:, xl, :])
                last.then_inc(s_lmv, 1)

            def conv_in(t, i, ps):
                v.transpose(cin[:, t * GT:(t + 1) * GT, 32 * i:32 * i + 32],
                            ps[:, :].rearrange("p (x g c) -> p g x c", x=XL, c=CG)).then_inc(s_cin, 1)

            def x_stats(b0, b1):
                for b in range(b0, b1):
                    if b % 4 == 0:
                        dve.wait_ge(s_x[b // 4], 16)
                    last = v.bn_stats(gstats[:, b, :], xin[:, b * NPOS:(b + 1) * NPOS])
                return last

            link(x_stats(0, B // 2))
            gn_aggregate(0, 0, B // 2)
            gn_variance(0, 0, B // 2, bank[7])
            gn_scale(0, 0, B // 2, bank[7])
            tap_rows()
            x_stats(B // 2, 3 * B // 4)
            for step in range(PAIRS + 3):
                work = []
                if 0 <= step - 3 < PAIRS:
                    def unit(t, i=step - 3):
                        u = 3 * i + t
                        dve.wait_ge(s_qkv, u + 1)
                        conv_in(t, i, bank[4 + u % 4])
                    work = [lambda t=t: unit(t) for t in range(3)]
                if step < PAIRS:
                    moments(step, bank[X_BANKS[step % 3]][:, :], None)
                for left in work:
                    left()
                if step == 0:
                    link(x_stats(3 * B // 4, B))
                    gn_aggregate(1, B // 2, B // 2)
                if step == 1:
                    gn_variance(1, B // 2, B // 2, bank[7])
                if step == 2:
                    gn_scale(1, B // 2, B // 2, bank[7])
                if step == 4:
                    dve.wait_ge(s_ident, 1)
                    small_masks()
                if step == PAIRS - 1:
                    fold_batchnorm()

            def conv_out(n):
                dve.wait_ge(s_grp, TSLOTS + 2 * (n + 1))
                for j in range(2):
                    t, g = divmod((2 * n + j) % NG, GT)
                    last = v.transpose(cpos[:, t, :, :, g * CG:(g + 1) * CG],
                                       bank[CONV_BANKS[n // (NG // 2)] + n % 2][:, j * B * HH:(j + 1) * B * HH])
                last.then_inc(s_ce, 1)

            def over_head(t):
                return t[:, :].unsqueeze(2).broadcast_to([P, PAIRS * XL, HD0])

            def q_shift(h):
                dve.wait_ge(s_ce, 2 + h + 1)
                if h:
                    dve.wait_ge(s_qs, h)
                link(v.tensor_reduce(qmax[:, :], head_q(h), op=ALU.max, axis=AX.X))
                v.tensor_tensor(head_q(h), head_q(h), over_head(qmax), ALU.subtract).then_inc(s_qs, 1)

            def q_scale(h):
                dve.wait_ge(s_qe, h + 1)
                if h:
                    dve.wait_ge(s_qn, h)
                link(v.tensor_reduce(qsum[:, :], head_q(h), op=ALU.add, axis=AX.X))
                link(v.reciprocal(qsum[:, :], qsum[:, :]))
                v.tensor_tensor(head_q(h), head_q(h), over_head(qsum), ALU.mult).then_inc(s_qn, 1)

            def k_max(i):
                dve.wait_ge(s_kq, i + 1)
                v.tensor_reduce(kneg[:, 2 * i:2 * i + 2],
                                bank[0][:, :].rearrange("p (n y b) -> p b n y", b=2, y=HH),
                                op=ALU.max, axis=AX.XY, negate=True).then_inc(s_kn, 1)

            dve.wait_ge(s_t0, 16 * WW)
            dve.wait_ge(s_t1, 16 * WW)
            heads = C // HD0
            for n in range(NG // 2):
                if n == NG // 2 - 2:
                    k_max(0)
                conv_out(n)
                if n >= 1 and (n - 1) % 2 == 0 and (n - 1) // 2 < heads:
                    q_shift((n - 1) // 2)
                if n >= 4 and n % 2 == 0 and (n - 4) // 2 < heads:
                    q_scale((n - 4) // 2)

            def ctx_mask(i):
                dve.wait_ge(s_ke, i + 1)
                link(v.reciprocal(krec[:, 2 * i:2 * i + 2], ksum[:, 2 * i:2 * i + 2]))
                dve.wait_ge(s_cx, i + 1)
                if i >= 2:
                    dve.wait_ge(s_o, i - 1)
                for b in range(2):
                    last = v.scalar_tensor_tensor(
                        out=ctxm[:, i % 2, b, 0:C], in0=bank[3][:, b * C:(b + 1) * C],
                        scalar=krec[:, 2 * i + b:2 * i + b + 1], in1=mask16[:, :], op0=ALU.mult, op1=ALU.mult)
                last.then_inc(s_cm, 1)

            def silu(i):
                dve.wait_ge(s_th, i + 1)
                v.scalar_tensor_tensor(out=ring_d[:, i % 2, :], in0=ring_d[:, i % 2, :], scalar=1.0,
                                       in1=bank[4][:, :], op0=ALU.add, op1=ALU.mult).then_inc(s_sl, 1)

            def x1(i):
                dve.wait_ge(s_zt, i + 1)
                dve.wait_ge(s_xp, i + 1)
                v.scalar_tensor_tensor(out=xres[:, i, :], in0=bank[7][:, :], scalar=vecs[:, 1:2],
                                       in1=xres[:, i, :], op0=ALU.mult, op1=ALU.add).then_inc(s_x1, 1)

            def x1_stats(i):
                dve.wait_ge(s_x1, i + 1)
                for b in range(2):
                    last = v.bn_stats(gstats[:, 2 * i + b, :], image(xres[:, i, :], b))
                for c, (i0, i1, _) in enumerate(GN1):
                    if i == i1 - 1:
                        link(last)
                        gn_aggregate(2 + c, 2 * i0, 2 * (i1 - i0))

            def kv_mask(n):
                dve.wait_ge(s_kv, n + 1)
                dve.wait_ge(s_o, PAIRS) if n < 2 else dve.wait_ge(s_num, n - 1)
                for b in range(2):
                    o = b * (C + 1)
                    v.tensor_tensor(ctxm[:, n % 2, b, 0:C], bank[4][:, o:o + C], mask8[:, :], ALU.mult)
                    last = v.tensor_scalar(ctxm[:, n % 2, b, C:C + NH1],
                                           mask8[:, :].rearrange("p (h d) -> p h d", d=HD1)[:, :, 0],
                                           bank[4][:, o + C:o + C + 1], None, ALU.mult)
                last.then_inc(s_kvm, 1)

            def attn_div(n):
                dve.wait_ge(s_num, n + 1)
                dve.wait_ge(s_zt, PAIRS) if n < 2 else dve.wait_ge(s_ot, n - 1)
                s = n % 2
                tiles = [bank[5 + b][:, 0:2 * (C + NH1)].rearrange("p (j c) -> p j c", j=2) for b in range(2)]
                for b in range(2):
                    last = v.tensor_scalar(den[:, s, b, :, :], tiles[b][:, :, C:C + NH1], ATT_EPS, None, ALU.add)
                link(last)
                dv = den[:, s, :, :, :].rearrange("p b j h -> p (b j h)")
                link(v.reciprocal(dv, dv))
                for b in range(2):
                    last = v.tensor_tensor(
                        ring_e[:, s, 2 * b * C:2 * (b + 1) * C].rearrange("p (j h d) -> p j h d", j=2, d=HD1),
                        tiles[b][:, :, 0:C].rearrange("p j (h d) -> p j h d", d=HD1),
                        den[:, s, b, :, :].unsqueeze(3).broadcast_to([P, 2, NH1, HD1]), ALU.mult)
                last.then_inc(s_div, 1)

            def low_parts(g):
                if g >= TSLOTS:
                    dve.wait_ge(s_grp, NG + g + 1)
                dve.wait_ge(s_hi, g + 1)
                for part, whole in ((cin_parts, cin[:, g, :]), (band_parts, tband[:, g % TSLOTS, :])):
                    last = v.tensor_tensor(part[:, g % TSLOTS, 1, :], whole,
                                           part[:, g % TSLOTS, 0, :].bitcast(F32), ALU.subtract)
                last.then_inc(s_lo, 1)

            dve.sem_inc(s_lo, TSLOTS)
            for step in range(FRONT1 + PAIRS + 3):
                work = []
                n = step - FRONT1
                if 0 <= step - 6 < PAIRS:
                    work.append(lambda: x1(step - 6))
                begun = 0
                for c, (i0, i1, at) in enumerate(GN1):
                    if step == at + 1 + (c == 0):
                        if 0 <= step - 4 < PAIRS:
                            begun = XL - 1
                            work[0:0] = [lambda xl=xl: tile_stats(PAIRS + step - 4, bank[5 + step % 2][:, :], xl)
                                         for xl in range(begun)]
                        gn_scale(2 + c, 2 * i0, 2 * (i1 - i0), gn_sums[c], work)
                if 0 <= step - 4 < PAIRS:
                    moments(PAIRS + step - 4, bank[5 + step % 2][:, :], work, begun)
                for left in work:
                    left()
                if 0 <= step - 3 < PAIRS:
                    silu(step - 3)
                if 0 <= step - 2 < PAIRS:
                    ctx_mask(step - 2)
                if 0 <= step - 6 < PAIRS:
                    x1_stats(step - 6)
                if 1 <= step < PAIRS:
                    k_max(step)
                if 0 <= n - 3 < PAIRS:
                    attn_div(n - 3)
                if 0 <= n - PAIRS - 1 < LOW_EARLY:
                    low_parts(n - PAIRS - 1)
                if 0 <= n - 2 < PAIRS:
                    kv_mask(n - 2)
                for c, (i0, i1, at) in enumerate(GN1):
                    if step == at:
                        gn_variance(2 + c, 2 * i0, 2 * (i1 - i0), gn_sums[c])
                if 0 <= n < PAIRS:
                    for t in range(3):
                        dve.wait_ge(s_qkv, 3 * PAIRS + 3 * n + t + 1)
                        conv_in(t, n, bank[t])

            def half0_low(i):
                dve.wait_ge(s_h0, i + 1)
                v.tensor_tensor(proj_parts[:, i % 2, 0, 1, :], half0[:, i, :],
                                proj_parts[:, i % 2, 0, 0, :].bitcast(F32), ALU.subtract).then_inc(s_p0, 1)

            for g in range(LOW_EARLY, 3):
                low_parts(g)
            for n in range(NG // 2, NG):
                for g in (2 * (n - NG // 2) + 3, 2 * (n - NG // 2) + 4):
                    if g < NG:
                        low_parts(g)
                if n == NG - 1:
                    dve.wait_ge(s_whi, 1)
                    v.tensor_tensor(w_parts[:, :, 1, :], wpt[:, :, :], w_parts[:, :, 0, :].bitcast(F32), ALU.subtract)
                    half0_low(0)
                conv_out(n)

            dve.wait_ge(s_ce, 2 + NG)
            dve.wait_ge(s_kv, PAIRS - 1)
            for b in range(2):
                last = v.tensor_scalar(ring_v[:, 0, b, :, 0:C], cpos[:, 2, 0], mask_b[:, b:b + 1], None, ALU.mult)
            last.then_inc(s_vfirst, 1)

            def y(i):
                dve.wait_ge(s_fin, i + 1)
                for b in range(2):
                    r = image(xres[:, i, :], b)
                    last = v.scalar_tensor_tensor(
                        out=r, in0=bank[2][:, b * NPOS:(b + 1) * NPOS].rearrange("p (n y) -> p n y", y=HH),
                        scalar=bn_bias[:, :], in1=r, op0=ALU.add, op1=ALU.add)
                last.then_inc(s_y, 1)

            def half1_low(i):
                dve.wait_ge(s_half, PAIRS + i + 1)
                v.tensor_tensor(proj_parts[:, i % 2, 1, 1, :], bank[7][:, :],
                                proj_parts[:, i % 2, 1, 0, :].bitcast(F32), ALU.subtract).then_inc(s_p1, 1)

            for step in range(PAIRS + 3):
                if 1 <= step - 2 < PAIRS:
                    half0_low(step - 2)
                if 0 <= step - 3 < PAIRS:
                    y(step - 3)
                if 0 <= step - 2 < PAIRS:
                    half1_low(step - 2)
                if 0 <= step - 1 < PAIRS:
                    attn_div(PAIRS + step - 1)
                if step < PAIRS:
                    kv_mask(PAIRS + step)

        @block.tensor
        def _(pe):
            t_ = nc.tensor

            def transposes(dst, src):
                for xl in range(XL):
                    last = t_.transpose(tile(dst, xl), src(xl), ident[:, :])
                return last

            def product(dst, stationary, moving, start=True, stop=True):
                return t_.matmul(dst, stationary, moving, start=start, stop=stop, skip_group_check=True)

            def gn_mean(c, k, b0, n, ps):
                pe.wait_ge(s_gnv, 2 * c + k + 1)
                product(ps[:, B * k:B * k + n], mean4[:, :], gmv[:, b0:b0 + n, k]).then_inc(s_gnp, 1)

            pe.sem_inc(s_grp, TSLOTS)
            pe.sem_inc(s_ce, 2)

            pe.wait_ge(s_const, 1)
            for k in range(2):
                gn_mean(0, k, 0, B // 2, bank[7])
            pe.wait_ge(s_ident, 1)
            pe.wait_ge(s_w0, 16 * 5)
            for n in range(4):
                last = t_.transpose(tile(bank[0], n), wst[n], ident[:, :])
            last.then_inc(s_wt, 1)
            pe.wait_ge(s_wte, 1)
            for step in range(PAIRS + 3):
                if step < PAIRS:
                    i = step
                    pe.wait_ge(s_xg, i + 1)
                    if i >= 3:
                        pe.wait_ge(s_nrm, i - 2)
                    transposes(bank[X_BANKS[i % 3]], lambda xl: tile(ring_a[:, i % 2, :], xl)).then_inc(s_xgt, 1)
                if 0 <= step - 2 < PAIRS:
                    i = step - 2
                    pe.wait_ge(s_nrm, i + 1)
                    if i >= 1:
                        pe.wait_ge(s_xn, i)
                    transposes(bank[2], lambda xl: tile(ring_b[:, i % 2, :], xl)).then_inc(s_nrm_t, 1)
                if 0 <= step - 3 < PAIRS:
                    i = step - 3
                    pe.wait_ge(s_xn, i + 1)
                    for t in range(3):
                        u = 3 * i + t
                        if u >= 4:
                            pe.wait_ge(s_cin, u - 3)
                        if u == 3:
                            pe.wait_ge(s_gn, 2)
                        for xl in range(XL):
                            last = product(tile(bank[4 + u % 4], xl), tile(ring_c[:, i % 2, :], xl),
                                           w0t[:, t * C:(t + 1) * C])
                        last.then_inc(s_qkv, 1)
                if step == 1:
                    gn_mean(1, 0, B // 2, B // 2, bank[7])
                if step == 2:
                    gn_mean(1, 1, B // 2, B // 2, bank[7])

            pe.wait_ge(s_nrm, PAIRS)
            pe.wait_ge(s_bnw, 1)
            pe.wait_ge(s_w, 16 * 8)
            pe.wait_ge(s_cin, 3 * PAIRS)
            for n in range(3):
                t_.transpose(tile(bank[4], n), wst[4 + n], ident[:, :])
            for n in range(3):
                product(tile(bank[0], n), pwrep[:, n].rearrange("p x c -> p (x c)"), ident[:, :])
            for n in range(2):
                last = t_.transpose(tile(bank[1], n), wst[7 + n], ident[:, :])
            last.then_inc(s_wt, 1)

            def conv0(it0, it1):
                order = [K0 // 2] + [k for k in range(K0) if k != K0 // 2]
                with pe.Fori(it0, it1) as it:
                    for j in range(TSLOTS):
                        ps = bank[CONV_BANKS[0] + j // 2]
                        dst = ps[:, (j % 2) * B * HH:(j % 2 + 1) * B * HH].rearrange("p (i n) -> p i n", i=PAIRS)
                        src = cin[:, bass.ds(it * TSLOTS + j, 1), :].rearrange("p g (i n) -> p (g i) n", i=PAIRS)
                        if j % 2 == 0:
                            pe.wait_ge(s_ce, it * 2 + (j // 2 + 1))
                        pe.wait_ge(s_tb, it * TSLOTS + (j + 1))
                        for k in order:
                            dy = k - K0 // 2
                            lo, hi = max(0, -dy), min(HH, HH - dy)
                            last = product(dst[:, :, 2 * lo:2 * hi], tband[:, j, k * C:(k + 1) * C],
                                           src[:, :, 2 * (lo + dy):2 * (hi + dy)],
                                           start=k == K0 // 2, stop=k == order[-1])
                        last.then_inc(s_grp, 1)

            def conv1_group(it, j):
                order = [K1 // 2] + [k for k in range(K1) if k != K1 // 2]
                ps = bank[CONV_BANKS[1] + j // 2]
                dst = ps[:, (j % 2) * B * HH:(j % 2 + 1) * B * HH].rearrange("p (i n) -> p i n", i=PAIRS)
                if j % 2 == 0:
                    pe.wait_ge(s_ce, it * 2 + (NG // 2 + j // 2 + 1))
                for q_band, q_in in ((0, 0), (0, 1), (1, 0)):
                    if (q_band, q_in) == (0, 0):
                        pe.wait_ge(s_hi, it * TSLOTS + (j + 1))
                    elif q_in:
                        pe.wait_ge(s_lo, it * TSLOTS + (TSLOTS + j + 1))
                    src = cin_parts[:, j, q_in, :].rearrange("p (i n) -> p i n", i=PAIRS)
                    for k in order:
                        dy = k - K1 // 2
                        lo, hi = max(0, -dy), min(HH, HH - dy)
                        last = product(dst[:, :, 2 * lo:2 * hi], band_parts[:, j, q_band, k * C:(k + 1) * C],
                                       src[:, :, 2 * (lo + dy):2 * (hi + dy)],
                                       start=(q_band, q_in, k) == (0, 0, K1 // 2),
                                       stop=q_band == 1 and k == order[-1])
                last.then_inc(s_grp, 1)

            def kq_transpose(i):
                if i == 0:
                    pe.wait_ge(s_ce, 2 + 2 * GT // 2)
                    pe.wait_ge(s_qn, C // HD0)
                    pe.wait_ge(s_wte, 2)
                else:
                    pe.wait_ge(s_ke, i)
                    pe.wait_ge(s_qc, i)
                transposes(bank[0], lambda xl: cpos[:, 1, i, xl])
                transposes(bank[1], lambda xl: cpos[:, 0, i, xl]).then_inc(s_kq, 1)

            pe.wait_ge(s_nrm, PAIRS)
            pe.wait_ge(s_cin, 3 * PAIRS)
            conv0(0, NG // TSLOTS - 1)
            kq_transpose(0)
            conv0(NG // TSLOTS - 1, NG // TSLOTS)

            def k_back(i):
                pe.wait_ge(s_ke, i + 1)
                if i == 0:
                    pe.wait_ge(s_ce, 2 + NG // 2)
                if i >= 1:
                    pe.wait_ge(s_kp, i)
                transposes(bank[2], lambda xl: tile(ring_a[:, i % 2, :], xl)).then_inc(s_kt, 1)

            def context(i):
                pe.wait_ge(s_kp, i + 1)
                pe.wait_ge(s_vm, i + 1)
                if i >= 1:
                    pe.wait_ge(s_cm, i)
                for xl in range(XL):
                    last = product(bank[3][:, 0:2 * C], tile(ring_c[:, i % 2, :], xl), ring_v[:, i % 2, :, xl, 0:C],
                                   start=xl == 0, stop=xl == XL - 1)
                last.then_inc(s_cx, 1)

            def attend(i):
                pe.wait_ge(s_cm, i + 1)
                pe.wait_ge(s_qc, i + 1)
                if i >= 1:
                    pe.wait_ge(s_sl, i)
                for b in range(2):
                    last = product(image(bank[4][:, :], b), ctxm[:, i % 2, b, 0:C], image(ring_b[:, i % 2, :], b))
                last.then_inc(s_o, 1)

            def project(i):
                pe.wait_ge(s_sl, i + 1)
                if i >= 2:
                    pe.wait_ge(s_nrm, PAIRS + i - 1)
                for xl in range(XL):
                    last = product(tile(bank[5 + i % 2], xl), tile(ring_d[:, i % 2, :], xl), owt[:, :])
                last.then_inc(s_pr, 1)

            def z_transpose(i):
                pe.wait_ge(s_nrm, PAIRS + i + 1)
                if i >= 1:
                    pe.wait_ge(s_x1, i)
                transposes(bank[7], lambda xl: tile(ring_e[:, i % 2, :], xl)).then_inc(s_zt, 1)

            def qkv1(i):
                pe.wait_ge(s_xg1, i + 1)
                w = w1t[:, :].rearrange("p (h t e) -> p t h e", t=3, e=HD1)
                for t, (free, free0) in enumerate(((s_q1, s_qc), (s_k1, s_kp), (s_v1, s_kp))):
                    if i == 0:
                        pe.wait_ge(s_ke, PAIRS)
                        pe.wait_ge(free0, PAIRS)
                    else:
                        pe.wait_ge(free, i)
                    for xl in range(XL):
                        last = product(tile(bank[t], xl), tile(ring_a[:, i % 2, :], xl), w[:, t])
                    last.then_inc(s_qkv, 1)

            def q_transpose1(n, src):
                if n == 0:
                    pe.wait_ge(s_cm, PAIRS)
                else:
                    pe.wait_ge(s_qc1, n)
                transposes(bank[3], src).then_inc(s_qt1, 1)

            def kv_product(n, k):
                pe.wait_ge(s_k1, n + 1)
                if n == PAIRS:
                    pe.wait_ge(s_vfirst, 1)
                else:
                    pe.wait_ge(s_v1, n + 1 if n < PAIRS else n)
                if n == 0:
                    pe.wait_ge(s_gn, 4)
                else:
                    pe.wait_ge(s_kvm, n)
                for xl in range(XL):
                    last = product(bank[4][:, 0:2 * (C + 1)], k(xl), ring_v[:, n % 2, :, xl, :],
                                   start=xl == 0, stop=xl == XL - 1)
                last.then_inc(s_kv, 1)

            def attend1(n):
                pe.wait_ge(s_kvm, n + 1)
                pe.wait_ge(s_qc1, n + 1)
                if n == 0:
                    pe.wait_ge(s_nrm, 2 * PAIRS)
                else:
                    pe.wait_ge(s_div, n)
                for b in range(2):
                    for j in range(2):
                        last = product(bank[5 + b][:, j * (C + NH1):(j + 1) * (C + NH1)],
                                       tile(ring_d[:, n % 2, :], 2 * b + j), ctxm[:, n % 2, b, :])
                last.then_inc(s_num, 1)

            def o_transpose(n):
                pe.wait_ge(s_div, n + 1)
                if n == 0:
                    pe.wait_ge(s_gn, 5)
                else:
                    pe.wait_ge(s_half, n) if n <= PAIRS else pe.wait_ge(s_p1, n - PAIRS)
                transposes(bank[7], lambda xl: tile(ring_e[:, n % 2, :], xl)).then_inc(s_ot, 1)

            for step in range(FRONT1 + PAIRS + 4):
                n = step - FRONT1
                for c, (i0, i1, at) in enumerate(GN1):
                    if c and step == at + 1:
                        gn_mean(2 + c, 1, 2 * i0, 2 * (i1 - i0), gn_sums[c])
                if 0 <= step - 6 < PAIRS:
                    z_transpose(step - 6)
                if 0 <= step - 4 < PAIRS:
                    project(step - 4)
                if 0 <= step - 3 < PAIRS:
                    attend(step - 3)
                if 0 <= step - 2 < PAIRS:
                    context(step - 2)
                if 0 <= step - 1 < PAIRS:
                    k_back(step - 1)
                if 1 <= step < PAIRS:
                    kq_transpose(step)
                for c, (i0, i1, at) in enumerate(GN1):
                    if step == at:
                        pe.wait_ge((s_ke, s_sl, s_x1)[c], PAIRS)
                        gn_mean(2 + c, 0, 2 * i0, 2 * (i1 - i0), gn_sums[c])
                if 0 <= n - 3 < PAIRS:
                    attend1(n - 3)
                if 0 <= n - 2 < PAIRS:
                    kv_product(n - 2, lambda xl: tile(ring_c[:, n % 2, :], xl))
                if 0 <= n - 1 < PAIRS:
                    pe.wait_ge(s_q1, n)
                    q_transpose1(n - 1, lambda xl: tile(ring_b[:, (n - 1) % 2, :], xl))
                if step == GN1[0][2] + 1:
                    gn_mean(2, 1, 0, 2 * GN1[0][1], gn_sums[0])
                if 0 <= n - 4 < PAIRS:
                    o_transpose(n - 4)
                if 0 <= n < PAIRS:
                    qkv1(n)
                for j, at in enumerate(CONV1_STEPS):
                    if n == at:
                        if j == 0:
                            pe.wait_ge(s_v1, PAIRS)
                        conv1_group(0, j)

            with pe.Fori(1, NG // TSLOTS) as it:
                for j in range(TSLOTS):
                    conv1_group(it, j)

            def final(i, half):
                pe.wait_ge((s_p0, s_p1)[half], i + 1)
                if i >= 1 and half == 0:
                    pe.wait_ge(s_y, i)
                for q_w, q_in in ((0, 0), (0, 1), (1, 0)):
                    last = product(bank[2][:, :], w_parts[:, half, q_w, :], proj_parts[:, i % 2, half, q_in, :],
                                   start=(half, q_w, q_in) == (0, 0, 0), stop=half == 1 and q_w == 1)
                if half == 1:
                    last.then_inc(s_fin, 1)

            for step in range(PAIRS + 3):
                if 0 <= step - 3 < PAIRS:
                    if step > 3:
                        final(step - 3, 0)
                    final(step - 3, 1)
                if 0 <= step - 2 < PAIRS:
                    o_transpose(PAIRS + step - 2)
                if step < PAIRS:
                    q_transpose1(PAIRS + step, lambda xl: cpos[:, 0, step, xl])
                if step == 0:
                    final(0, 0)
                if 0 <= step - 1 < PAIRS:
                    attend1(PAIRS + step - 1)
                if step < PAIRS:
                    kv_product(PAIRS + step, lambda xl: cpos[:, 1, step, xl])


_INS = ["x", "L0_conv_g_norm", "L0_conv_q_w1", "L0_conv_q_dw", "L0_conv_k_w1", "L0_conv_k_dw", "L0_conv_v_w1",
        "L0_conv_v_dw", "L0_conv_out_w", "L0_conv_g_out", "L1_conv_w_qkv", "L1_conv_w_dw", "L1_conv_w_pw",
        "L1_conv_w_proj", "L1_conv_bn_gamma", "L1_conv_bn_beta", "L1_conv_bn_mean", "L1_conv_bn_var"]


def kernel(**inputs):
    import numpy as _np
    import concourse.bacc as _bacc
    from concourse import mybir as _mybir
    from concourse.bass_utils import run_bass_kernel_spmd as _run

    nc = _bacc.Bacc("TRN2", target_bir_lowering=False, num_devices=1)
    arrays, args = {}, []
    for name in _INS:
        a = _np.ascontiguousarray(inputs[name])
        arrays[f"in_{name}_dram"] = a
        args.append(nc.dram_tensor(f"in_{name}_dram", a.shape, _mybir.dt.from_np(a.dtype), kind="ExternalInput").ap())
    shape = inputs["x"].shape
    args.append(nc.dram_tensor("out_dram", shape, _mybir.dt.float32, kind="ExternalOutput").ap())
    conv_blocks_kernel(nc, *args)
    r = _run(nc, [arrays], core_ids=[0])
    return r.results[0]["out_dram"]
```
